# Optimizing a Trainium2 kernel written in Bass

```python
import numpy as np
import jax
import jax.numpy as jnp

def _softmax(x, axis=-1):
    return jax.nn.softmax(x, axis=axis)

def _gelu(x):
    return jax.nn.gelu(x, approximate=True)

def _silu(x):
    return jax.nn.silu(x)

def _sigmoid(x):
    return jax.nn.sigmoid(x)

def _layernorm(x, axis=-1, eps=1e-05):
    m = jnp.mean(x, axis=axis, keepdims=True)
    v = jnp.var(x, axis=axis, keepdims=True)
    return (x - m) / jnp.sqrt(v + eps)

def _scatter_add(tgt, idx, src, axis=0):
    return tgt.at[idx].add(src)

def _segment_sum(src, seg, n):
    return jax.ops.segment_sum(src, seg, n)
kernel_name = 'mk_vit_tower_d1_tok_img512_r4_ce720e'

def setup_inputs(seed: int=0):
    np.random.seed(seed)
    _w = jnp.asarray

    def _rec_inputs():
        import jax
        import jax.numpy as jnp
        _rk = jax.random.key(seed)
        x = -0.000222058 + 0.999998 * jax.random.normal(jax.random.fold_in(_rk, 1), (32, 3, 64, 64), jnp.float32)
        return x
    x = _rec_inputs()

    def _L0_tok_setup():
        import jax, jax.numpy as jnp
        import numpy as np
        IMG, P, C, D = (64, 16, 3, 128)
        NP = (IMG // P) ** 2
        PD = P * P * C
        key = jax.random.key(seed)
        k1, k2, k3 = jax.random.split(key, 3)
        x = jax.random.normal(k1, (128, C, IMG, IMG), dtype=jnp.float32)
        W = jax.random.normal(k2, (D, PD), dtype=jnp.float32) * (1.0 / np.sqrt(PD))
        b = jax.random.normal(k3, (D,), dtype=jnp.float32) * 0.01
        return {'x': x, 'W': W, 'b': b}
    _L0_tok_all = _L0_tok_setup()
    _L0_tok_in = {k: v for k, v in _L0_tok_all.items() if k in ('W', 'b')}
    del _L0_tok_all

    def _L0_attn_setup():
        import jax, jax.numpy as jnp
        import numpy as np
        D_MODEL = 128
        N = 64
        L_MAX = 512
        BATCH = 8
        DT = 0.1

        def _compute_kernel(L_param, P_left, P_right, B, C, log_dt):
            I = jnp.eye(N, dtype=L_param.dtype)
            L_mat = I * jnp.exp(L_param)[:, None, :]
            P = jnp.einsum('dnk,dkm->dnm', P_left, P_right)
            A = -L_mat + P
            dt = jnp.exp(log_dt)
            A = A * dt[..., None]
            Bd = B * dt
            M = I - A / 2
            dA = jnp.linalg.solve(M, I + A / 2)
            dB = jnp.linalg.solve(M, Bd[..., None])[..., 0]

            def step(state, _):
                k_t = jnp.einsum('dn,dn->d', C, state)
                new_state = jnp.einsum('dnm,dm->dn', dA, state)
                return (new_state, k_t)
            _, k = jax.lax.scan(step, dB, None, length=L_MAX)
            return k.T
        key = jax.random.key(seed)
        ks = jax.random.split(key, 6)
        x = jax.random.normal(ks[0], (BATCH, L_MAX, D_MODEL), dtype=jnp.float32)
        L_param = jnp.full((D_MODEL, N), 0.5, dtype=jnp.float32)
        P_left = 0.01 * jax.random.normal(ks[1], (D_MODEL, N, 2), dtype=jnp.float32)
        P_right = 0.01 * jax.random.normal(ks[2], (D_MODEL, 2, N), dtype=jnp.float32)
        B = jax.random.normal(ks[3], (D_MODEL, N), dtype=jnp.float32) / np.sqrt(N).astype(np.float32)
        C = jax.random.normal(ks[4], (D_MODEL, N), dtype=jnp.float32) / np.sqrt(N).astype(np.float32)
        D = jnp.ones((D_MODEL,), dtype=jnp.float32)
        log_dt = jnp.log(DT * jnp.ones((D_MODEL, 1), dtype=jnp.float32))
        return {'x': x, 'L_param': L_param, 'P_left': P_left, 'P_right': P_right, 'B': B, 'C': C, 'D': D, 'log_dt': log_dt}
    _L0_attn_all = _L0_attn_setup()
    _L0_attn_in = {k: v for k, v in _L0_attn_all.items() if k in ('L_param', 'P_left', 'P_right', 'B', 'C', 'D', 'log_dt')}
    del _L0_attn_all

    def _L0_ffn_setup():
        import jax, jax.numpy as jnp
        import numpy as np
        K_INPUT, K_PROCESS, K_OUTPUT = (64, 128, 64)

        def _gelu(x):
            return jax.nn.gelu(x, approximate=False)
        key = jax.random.key(seed)
        ks = jax.random.split(key, 6)
        d_model, n_in, n_proc, n_out, d_pv = (128, 512, 256, 512, 64)
        B, S = (2, 256)

        def xavier(k, shape):
            std = (2.0 / (shape[0] + shape[1])) ** 0.5
            return jax.random.normal(k, shape, dtype=jnp.float32) * std
        return {'x': jax.random.normal(ks[0], (B, S, d_model), dtype=jnp.float32), 'input_patterns': xavier(ks[1], (n_in, d_model)), 'process_input_weights': xavier(ks[2], (n_proc, n_in)), 'process_values': xavier(ks[3], (n_proc, d_pv)), 'output_input_weights': xavier(ks[4], (n_out, d_pv)), 'output_patterns': xavier(ks[5], (n_out, d_model))}
    _L0_ffn_all = _L0_ffn_setup()
    _L0_ffn_in = {k: v for k, v in _L0_ffn_all.items() if k in ('input_patterns', 'process_input_weights', 'process_values', 'output_input_weights', 'output_patterns')}
    del _L0_ffn_all
    return {'x': x, 'L0_tok_W': _L0_tok_in['W'], 'L0_tok_b': _L0_tok_in['b'], 'L0_attn_L_param': _L0_attn_in['L_param'], 'L0_attn_P_left': _L0_attn_in['P_left'], 'L0_attn_P_right': _L0_attn_in['P_right'], 'L0_attn_B': _L0_attn_in['B'], 'L0_attn_C': _L0_attn_in['C'], 'L0_attn_D': _L0_attn_in['D'], 'L0_attn_log_dt': _L0_attn_in['log_dt'], 'L0_ffn_input_patterns': _L0_ffn_in['input_patterns'], 'L0_ffn_process_input_weights': _L0_ffn_in['process_input_weights'], 'L0_ffn_process_values': _L0_ffn_in['process_values'], 'L0_ffn_output_input_weights': _L0_ffn_in['output_input_weights'], 'L0_ffn_output_patterns': _L0_ffn_in['output_patterns']}

def reference(x, L0_tok_W, L0_tok_b, L0_attn_L_param, L0_attn_P_left, L0_attn_P_right, L0_attn_B, L0_attn_C, L0_attn_D, L0_attn_log_dt, L0_ffn_input_patterns, L0_ffn_process_input_weights, L0_ffn_process_values, L0_ffn_output_input_weights, L0_ffn_output_patterns):
    import jax
    import jax.numpy as jnp

    def _L0_tok_ref(x, W, b):
        import jax, jax.numpy as jnp
        import numpy as np
        IMG, P, C, D = (64, 16, 3, 128)
        NP = (IMG // P) ** 2
        PD = P * P * C
        B, c, H, Wd = x.shape
        xp = x.reshape(B, c, H // P, P, Wd // P, P)
        xp = xp.transpose(0, 2, 4, 1, 3, 5).reshape(B, NP, c * P * P)
        return jnp.einsum('bnk,dk->bnd', xp, W) + b

    def _L0_attn_ref(x, L_param, P_left, P_right, B, C, D, log_dt):
        import jax, jax.numpy as jnp
        import numpy as np
        D_MODEL = 128
        N = 64
        L_MAX = 512
        BATCH = 8
        DT = 0.1

        def _compute_kernel(L_param, P_left, P_right, B, C, log_dt):
            I = jnp.eye(N, dtype=L_param.dtype)
            L_mat = I * jnp.exp(L_param)[:, None, :]
            P = jnp.einsum('dnk,dkm->dnm', P_left, P_right)
            A = -L_mat + P
            dt = jnp.exp(log_dt)
            A = A * dt[..., None]
            Bd = B * dt
            M = I - A / 2
            dA = jnp.linalg.solve(M, I + A / 2)
            dB = jnp.linalg.solve(M, Bd[..., None])[..., 0]

            def step(state, _):
                k_t = jnp.einsum('dn,dn->d', C, state)
                new_state = jnp.einsum('dnm,dm->dn', dA, state)
                return (new_state, k_t)
            _, k = jax.lax.scan(step, dB, None, length=L_MAX)
            return k.T
        batch, L, _ = x.shape
        xt = jnp.transpose(x, (0, 2, 1))
        kernel = _compute_kernel(L_param, P_left, P_right, B, C, log_dt)
        n_fft = 2 * L_MAX
        kf = jnp.fft.rfft(kernel, n=n_fft)
        xf = jnp.fft.rfft(xt, n=n_fft)
        y = jnp.fft.irfft(xf * kf, n=n_fft)[..., :L]
        y = y + D[None, :, None] * xt
        return jnp.transpose(y, (0, 2, 1))

    def _L0_ffn_ref(x, input_patterns, process_input_weights, process_values, output_input_weights, output_patterns):
        import jax, jax.numpy as jnp
        import numpy as np
        K_INPUT, K_PROCESS, K_OUTPUT = (64, 128, 64)

        def _gelu(x):
            return jax.nn.gelu(x, approximate=False)
        B, S, d_model = x.shape
        n_in = input_patterns.shape[0]
        input_acts = _gelu(jnp.einsum('bsd,nd->bsn', x, input_patterns))
        top_in_acts, top_in_idx = jax.lax.top_k(input_acts, K_INPUT)
        bi = jnp.arange(B)[:, None, None]
        si = jnp.arange(S)[None, :, None]
        input_repr = jnp.zeros((B, S, n_in), dtype=x.dtype).at[bi, si, top_in_idx].set(top_in_acts)
        process_acts = _gelu(jnp.einsum('bsn,pn->bsp', input_repr, process_input_weights))
        top_p_acts, top_p_idx = jax.lax.top_k(process_acts, K_PROCESS)
        sel_values = process_values[top_p_idx]
        p_weights = jax.nn.softmax(top_p_acts, axis=-1)
        agg_value = jnp.einsum('bsk,bskd->bsd', p_weights, sel_values)
        output_acts = _gelu(jnp.einsum('bsd,od->bso', agg_value, output_input_weights))
        top_o_acts, top_o_idx = jax.lax.top_k(output_acts, K_OUTPUT)
        sel_patterns = output_patterns[top_o_idx]
        out = jnp.einsum('bsk,bskm->bsm', top_o_acts, sel_patterns)
        return out
    h = _L0_tok_ref(x, L0_tok_W, L0_tok_b)
    h = h + _L0_attn_ref(_layernorm(h, axis=-1), L0_attn_L_param, L0_attn_P_left, L0_attn_P_right, L0_attn_B, L0_attn_C, L0_attn_D, L0_attn_log_dt)
    h = h + _L0_ffn_ref(_layernorm(h, axis=-1), L0_ffn_input_patterns, L0_ffn_process_input_weights, L0_ffn_process_values, L0_ffn_output_input_weights, L0_ffn_output_patterns)
    return h

_drawn_inputs = setup_inputs


def setup_inputs(seed=0):
    import zlib

    import numpy as np

    out = dict(_drawn_inputs(seed))
    spreads = {'L0_attn_L_param': (0.5, 0.6),
     'L0_attn_D': (1.0, 0.2),
     'L0_attn_log_dt': (-2.3025851249694824, 0.6)}
    factors = {'L0_tok_b': 5.655,
     'L0_attn_P_left': 8.0,
     'L0_attn_P_right': 8.0,
     'L0_attn_B': 5.643,
     'L0_attn_C': 6.662,
     'L0_ffn_input_patterns': 8.0,
     'L0_ffn_process_input_weights': 8.0,
     'L0_ffn_process_values': 8.0,
     'L0_ffn_output_input_weights': 8.0,
     'L0_ffn_output_patterns': 8.0}
    for name, (base, spread) in spreads.items():
        noise = np.random.default_rng([zlib.crc32(name.encode()), seed]).standard_normal(out[name].shape)
        drawn = base * np.exp(spread * noise) if base else spread * noise
        out[name] = jnp.asarray(drawn.astype(out[name].dtype))
    for name, factor in factors.items():
        out[name] = (out[name] * factor).astype(out[name].dtype)
    return out
```

```python
import concourse.bass as bass
from concourse import mybir
from contextlib import ExitStack

FP32 = mybir.dt.float32
ALU = mybir.AluOpType
ACT = mybir.ActivationFunctionType
AX = mybir.AxisListType

P = 128
BATCH = 32
PATCHES = 16
TOK = BATCH * PATCHES
TILES = TOK // P
IMGS = P // PATCHES
KC = 6
STATE = 64
TAPS = PATCHES
N_IN, N_PROC, N_OUT, D_PV = 512, 256, 512, 64
K_IN, K_PROC, K_OUT = 64, 128, 64
EPS = 1e-5
LOW = -3.0e38
PICKED = -1.0e38
C_L, C_PL, C_PR, C_B, C_C = 0, STATE, 3 * STATE, 5 * STATE, 6 * STATE
C_D, C_DT = 7 * STATE, 7 * STATE + 1
SSM_COLS = 7 * STATE + 2


def build(nc, x_t, w_t, tok_b, ssm, ip_t, piw_t, pv, oiw_t, op, out):
    ctx = ExitStack()
    with ctx:
        def sb(name, shape):
            return ctx.enter_context(nc.sbuf_tensor(name, shape, FP32))

        def pb(name, shape):
            return ctx.enter_context(nc.psum_tensor(name, shape, FP32))

        def sem(name):
            return ctx.enter_context(nc.semaphore(name))

        xt = sb("xt", [P, TILES, KC, P])
        wt = sb("wt", [P, KC, P])
        brow = sb("brow", [1, P])
        par = sb("par", [P, SSM_COLS])
        ipt = sb("ipt", [P, N_IN])
        piwt = sb("piwt", [P, N_IN // P, N_PROC])
        pvs = sb("pvs", [P, N_PROC // P, D_PV])
        oiwt = sb("oiwt", [D_PV, N_OUT])
        ops = sb("ops", [P, N_OUT // P, P])
        ident = sb("ident", [P, P])
        ones = sb("ones", [1, P])
        minus_half = sb("minus_half", [P, TILES])
        el = sb("el", [P, STATE])
        dt = sb("dt", [P, 1])
        hdt = sb("hdt", [P, 1])
        g = sb("g", [P, STATE])
        omg = sb("omg", [P, STATE])
        ig = sb("ig", [P, STATE])
        a_diag = sb("a_diag", [P, STATE])
        xu = sb("xu", [P, 2, STATE])
        yv = sb("yv", [P, 2, STATE])
        vx = sb("vx", [P, 4])
        det = sb("det", [P, 4])
        inv = sb("inv", [P, 4])
        xh = sb("xh", [P, 2, STATE])
        xf = sb("xf", [P, 2, STATE])
        bi = sb("bi", [P, STATE])
        junk = sb("junk", [P, 2, STATE])
        wdot = sb("wdot", [P, 2])
        as_ = sb("as_", [P, STATE])
        as1 = sb("as1", [P, STATE])
        states = sb("states", [P, TAPS, STATE])
        cs = sb("cs", [P, TAPS, STATE])
        csum = sb("csum", [P, STATE])
        taps = sb("taps", [P, TAPS])
        tap_diag = sb("tap_diag", [P, TAPS, P])
        h_sb = sb("h_sb", [P, TILES, P])
        stats = sb("stats", [P, 2 * TILES, 6])
        mv = sb("mv", [P, 2 * TILES, 2])
        vare = sb("vare", [P, 2 * TILES])
        rstd = sb("rstd", [P, 2 * TILES])
        xn = sb("xn", [P, TILES, P])
        xnt = sb("xnt", [P, TILES, P])
        yt = sb("yt", [P, TILES, P])
        h2 = sb("h2", [P, TILES, P])
        xn2 = sb("xn2", [P, TILES, P])
        xn2t = sb("xn2t", [P, TILES, P])
        g1 = sb("g1", [P, TILES, N_IN])
        g2 = sb("g2", [P, TILES, N_PROC])
        g3 = sb("g3", [P, TILES, N_OUT])
        left = sb("left", [P, N_IN])
        v8 = sb("v8", [P, 8])
        top1 = sb("top1", [P, TILES, 8])
        nmax = sb("nmax", [P, TILES])
        e2 = sb("e2", [P, TILES, N_PROC])
        r1 = sb("r1", [P, TILES, N_IN])
        rt = sb("rt", [P, 2, N_IN])
        p2 = sb("p2", [P, TILES, N_PROC])
        psum_p = sb("psum_p", [P, TILES])
        rsum = sb("rsum", [P, TILES])
        aggt = sb("aggt", [D_PV, TILES, P])
        o_sb = sb("o_sb", [P, TILES, P])

        ps_q = [pb(f"ps_q{i}", [P, N_PROC * 2]) for i in range(2)]
        ps_t = [pb(f"ps_t{i}", [P, 4, P]) for i in range(2)]
        ps_y = pb("ps_y", [P, N_PROC * 2])
        ps_z = [pb(f"ps_z{i}", [P, N_IN]) for i in range(2)]
        ps_o = pb("ps_o", [P, N_PROC * 2])

        s_par = sem("s_par")
        s_w = sem("s_w")
        s_x = [sem(f"s_x{t}") for t in range(TILES)]
        s_ip, s_piw, s_pv, s_oiw, s_op = (sem(n) for n in ("s_ip", "s_piw", "s_pv", "s_oiw", "s_op"))
        s_id0, s_id = sem("s_id0"), sem("s_id")
        s_const = sem("s_const")
        s_exp = sem("s_exp")
        s_state = sem("s_state")
        s_cs = sem("s_cs")
        s_as = sem("s_as")
        s_csum = sem("s_csum")
        s_tap0 = sem("s_tap0")
        s_diag = sem("s_diag")
        s_h = sem("s_h")
        s_hsb = sem("s_hsb")
        s_var = sem("s_var")
        s_rstd = sem("s_rstd")
        s_xn = sem("s_xn")
        s_tp = sem("s_tp")
        s_xnt = sem("s_xnt")
        s_yt = sem("s_yt")
        s_ytsb = sem("s_ytsb")
        s_y = sem("s_y")
        s_xn2 = sem("s_xn2")
        s_h2 = sem("s_h2")
        s_xn2t = sem("s_xn2t")
        s_z1, s_z2, s_z3 = sem("s_z1"), sem("s_z2"), sem("s_z3")
        s_g1, s_g2, s_g3 = sem("s_g1"), sem("s_g2"), sem("s_g3")
        s_r1, s_p2, s_r3 = sem("s_r1"), sem("s_p2"), sem("s_r3")
        s_e2 = sem("s_e2")
        s_max = sem("s_max")
        s_nmax = sem("s_nmax")
        s_rt = sem("s_rt")
        s_agg = sem("s_agg")
        s_aggt = sem("s_aggt")
        s_rsum = sem("s_rsum")
        s_o = sem("s_o")
        s_osb = sem("s_osb")
        s_out = sem("s_out")
        s_dve = sem("s_dve")
        s_pool = sem("s_pool")

        block = ctx.enter_context(nc.Block())

        @block.sync
        def _(sp):
            sp.dma_start(par[:, :], ssm).then_inc(s_par, 16)
            for t in range(TILES):
                sp.dma_start(xt[:, t, :, :], x_t[t]).then_inc(s_x[t], 16)
            for t in range(TILES):
                sp.wait_ge(s_osb, t + 1)
                sp.dma_start(out[t], o_sb[:, t, :]).then_inc(s_out, 16)
            sp.wait_ge(s_out, 16 * TILES)

        @block.gpsimd
        def _(pool):
            nc.gpsimd.memset(ident[:, :], 0.0).then_inc(s_id0, 1)
            nc.gpsimd.memset(ones[:, :], 1.0).then_inc(s_const, 1)
            nc.gpsimd.memset(minus_half[:, :], -0.5).then_inc(s_pool, 1)
            pool.wait_ge(s_id0, 1)
            nc.gpsimd.affine_select(out=ident[:, :], in_=ident[:, :], compare_op=ALU.not_equal, fill=1.0,
                                    base=0, pattern=[[-1, P]], channel_multiplier=1).then_inc(s_id, 1)
            pool.wait_ge(s_par, 16)
            for k in range(TAPS):
                pool.wait_ge(s_state, k + 1)
                nc.gpsimd.tensor_tensor(cs[:, k, :], par[:, C_C:C_C + STATE], states[:, k, :],
                                        ALU.mult).then_inc(s_cs, 1)
            pool.wait_ge(s_pool, 1)
            for n in range(2 * TILES):
                pool.wait_ge(s_var, n + 1)
                nc.gpsimd.tensor_tensor(rstd[:, n:n + 1], vare[:, n:n + 1], minus_half[:, 0:1],
                                        ALU.pow).then_inc(s_rstd, 1)

        @block.scalar
        def _(act):
            act.dma_start(wt[:, :, :], w_t).then_inc(s_w, 16)
            act.dma_start(brow[:, :], tok_b).then_inc(s_w, 16)
            act.dma_start(ipt[:, :], ip_t).then_inc(s_ip, 16)
            act.dma_start(piwt[:, :, :], piw_t).then_inc(s_piw, 16)
            act.dma_start(pvs[:, :, :], pv).then_inc(s_pv, 16)
            act.dma_start(oiwt[:, :], oiw_t).then_inc(s_oiw, 16)
            act.dma_start(ops[:, :, :], op).then_inc(s_op, 16)
            act.wait_ge(s_par, 16)
            nc.scalar.activation(el[:, :], par[:, C_L:C_L + STATE], ACT.Exp).then_inc(s_exp, 1)
            nc.scalar.activation(dt[:, :], par[:, C_DT:C_DT + 1], ACT.Exp).then_inc(s_exp, 1)
            act.wait_ge(s_id, 1)
            for k in range(TAPS):
                act.wait_ge(s_cs, k + 1)
                nc.scalar.activation(csum[:, :], cs[:, k, :], ACT.Identity,
                                     accum_out=taps[:, k:k + 1]).then_inc(s_csum, 1)
                act.wait_ge(s_csum, k + 1)
                if k == 0:
                    nc.scalar.activation(taps[:, 0:1], taps[:, 0:1], ACT.Identity,
                                         bias=par[:, C_D:C_D + 1]).then_inc(s_tap0, 1)
                    act.wait_ge(s_tap0, 1)
                nc.scalar.activation(tap_diag[:, k, :], ident[:, :], ACT.Copy,
                                     scale=taps[:, k:k + 1]).then_inc(s_diag, 1)
            for t in range(TILES):
                act.wait_ge(s_h, t + 1)
                nc.scalar.activation(h_sb[:, t, :], ps_q[t % 2][:, 0:P], ACT.Copy).then_inc(s_hsb, 1)
            for t in range(TILES):
                act.wait_ge(s_tp, t + 1)
                nc.scalar.activation(xnt[:, t, :], ps_t[t % 2][:, 0, :], ACT.Copy).then_inc(s_xnt, 1)
                act.wait_ge(s_yt, t + 1)
                nc.scalar.activation(yt[:, t, :], ps_y[:, 0:P], ACT.Copy).then_inc(s_ytsb, 1)
            for t in range(TILES):
                act.wait_ge(s_tp, TILES + t + 1)
                nc.scalar.activation(xn2t[:, t, :], ps_t[t % 2][:, 0, :], ACT.Copy).then_inc(s_xn2t, 1)
                act.wait_ge(s_z1, t + 1)
                nc.scalar.activation(g1[:, t, :], ps_z[t % 2][:, :], ACT.Gelu).then_inc(s_g1, 1)
            for t in range(TILES):
                act.wait_ge(s_tp, 2 * TILES + t + 1)
                nc.scalar.activation(rt[:, t % 2, :], ps_t[t % 2][:, :, :], ACT.Copy).then_inc(s_rt, 1)
                act.wait_ge(s_z2, t + 1)
                nc.scalar.activation(g2[:, t, :], ps_q[t % 2][:, 0:N_PROC], ACT.Gelu).then_inc(s_g2, 1)
            for t in range(TILES):
                act.wait_ge(s_max, t + 1)
                nc.scalar.mul(nmax[:, t:t + 1], top1[:, t, 0:1], -1.0).then_inc(s_nmax, 1)
                act.wait_ge(s_nmax, t + 1)
                act.wait_ge(s_g2, t + 1)
                nc.scalar.activation(e2[:, t, :], g2[:, t, :], ACT.Exp, bias=nmax[:, t:t + 1]).then_inc(s_e2, 1)
            for t in range(TILES):
                act.wait_ge(s_tp, 3 * TILES + t + 1)
                nc.scalar.activation(rt[:, t % 2, 0:N_PROC], ps_t[t % 2][:, 0:2, :], ACT.Copy).then_inc(s_rt, 1)
                act.wait_ge(s_agg, t + 1)
                nc.scalar.activation(aggt[:, t, :], ps_y[0:D_PV, 0:P], ACT.Copy).then_inc(s_aggt, 1)
                act.wait_ge(s_z3, t + 1)
                act.wait_ge(s_rsum, t + 1)
                nc.scalar.activation(g3[:, t, :], ps_z[t % 2][:, :], ACT.Gelu,
                                     scale=rsum[:, t:t + 1]).then_inc(s_g3, 1)
            for t in range(TILES):
                act.wait_ge(s_tp, 4 * TILES + t + 1)
                nc.scalar.activation(rt[:, t % 2, :], ps_t[t % 2][:, :, :], ACT.Copy).then_inc(s_rt, 1)

        @block.vector
        def _(dve):
            chain = [0]

            def link(ins):
                chain[0] += 1
                ins.then_inc(s_dve, 1)
                dve.wait_ge(s_dve, chain[0])

            V = nc.vector
            vr = par[:, C_PR:C_PR + 2 * STATE].rearrange("p (i n) -> p i n", i=2)
            pl = par[:, C_PL:C_PL + 2 * STATE].rearrange("p (i n) -> p i n", i=2)

            def dot(out, u, v):
                return V.scalar_tensor_tensor(out=junk[:, 0, :], in0=u, scalar=1.0, in1=v, op0=ALU.mult,
                                              op1=ALU.mult, accum_out=out)

            dve.wait_ge(s_par, 16)
            dve.wait_ge(s_exp, 2)
            link(V.tensor_scalar(hdt[:, :], dt[:, :], 0.5, None, ALU.mult))
            link(V.tensor_scalar(g[:, :], el[:, :], hdt[:, 0:1], None, ALU.mult))
            link(V.tensor_scalar(omg[:, :], g[:, :], -1.0, 1.0, ALU.mult, ALU.add))
            link(V.tensor_scalar(g[:, :], g[:, :], 1.0, None, ALU.add))
            link(V.reciprocal(ig[:, :], g[:, :]))
            link(V.tensor_tensor(a_diag[:, :], omg[:, :], ig[:, :], ALU.mult))
            for i in range(2):
                link(V.scalar_tensor_tensor(out=xu[:, i, :], in0=pl[:, i, :], scalar=hdt[:, 0:1], in1=ig[:, :],
                                            op0=ALU.mult, op1=ALU.mult))
                link(V.tensor_tensor(yv[:, i, :], vr[:, i, :], ig[:, :], ALU.mult))
            link(V.scalar_tensor_tensor(out=bi[:, :], in0=par[:, C_B:C_B + STATE], scalar=dt[:, 0:1], in1=ig[:, :],
                                        op0=ALU.mult, op1=ALU.mult))
            for i in range(2):
                for j in range(2):
                    link(dot(vx[:, 2 * i + j:2 * i + j + 1], vr[:, i, :], xu[:, j, :]))
                link(dot(wdot[:, i:i + 1], vr[:, i, :], bi[:, :]))
            link(V.tensor_scalar(inv[:, :], vx[:, :], -1.0, 1.0, ALU.mult, ALU.add))
            link(V.tensor_tensor(det[:, 0:1], inv[:, 0:1], inv[:, 3:4], ALU.mult))
            link(V.tensor_tensor(det[:, 1:2], vx[:, 1:2], vx[:, 2:3], ALU.mult))
            link(V.tensor_tensor(det[:, 2:3], det[:, 0:1], det[:, 1:2], ALU.subtract))
            link(V.reciprocal(det[:, 3:4], det[:, 2:3]))
            for j in range(2):
                top = inv[:, 3:4] if j == 0 else vx[:, 1:2]
                bottom = vx[:, 2:3] if j == 0 else inv[:, 0:1]
                link(V.tensor_scalar(xf[:, 0, :], xu[:, 0, :], top, det[:, 3:4], ALU.mult, ALU.mult))
                link(V.tensor_scalar(xf[:, 1, :], xu[:, 1, :], bottom, det[:, 3:4], ALU.mult, ALU.mult))
                link(V.tensor_tensor(xh[:, j, :], xf[:, 0, :], xf[:, 1, :], ALU.add))
            link(V.scalar_tensor_tensor(out=as1[:, :], in0=xh[:, 0, :], scalar=wdot[:, 0:1], in1=bi[:, :],
                                        op0=ALU.mult, op1=ALU.add))
            link(V.tensor_scalar(xf[:, :, :], xh[:, :, :], 2.0, None, ALU.mult))
            V.scalar_tensor_tensor(out=states[:, 0, :], in0=xh[:, 1, :], scalar=wdot[:, 1:2], in1=as1[:, :],
                                   op0=ALU.mult, op1=ALU.add).then_inc(s_state, 1)
            for k in range(1, TAPS):
                dve.wait_ge(s_state, k)
                s = states[:, k - 1, :]
                link(dot(wdot[:, 0:1], yv[:, 0, :], s))
                link(dot(wdot[:, 1:2], yv[:, 1, :], s))
                link(V.tensor_tensor(as_[:, :], a_diag[:, :], s, ALU.mult))
                link(V.scalar_tensor_tensor(out=as1[:, :], in0=xf[:, 0, :], scalar=wdot[:, 0:1], in1=as_[:, :],
                                            op0=ALU.mult, op1=ALU.add))
                V.scalar_tensor_tensor(out=states[:, k, :], in0=xf[:, 1, :], scalar=wdot[:, 1:2], in1=as1[:, :],
                                       op0=ALU.mult, op1=ALU.add).then_inc(s_state, 1)

            def norm_stats(n, src):
                link(V.bn_stats(out=stats[:, n, :], in_=src))
                link(V.bn_aggr(out=mv[:, n, :], in_=stats[:, n, :]))
                V.tensor_scalar(vare[:, n:n + 1], mv[:, n, 1:2], EPS, None, ALU.add).then_inc(s_var, 1)

            for t in range(TILES):
                dve.wait_ge(s_hsb, t + 1)
                norm_stats(t, h_sb[:, t, :])
            for t in range(TILES):
                dve.wait_ge(s_rstd, t + 1)
                V.tensor_scalar(xn[:, t, :], h_sb[:, t, :], mv[:, t, 0:1], rstd[:, t:t + 1],
                                ALU.subtract, ALU.mult).then_inc(s_xn, 1)
            for t in range(TILES):
                n = TILES + t
                dve.wait_ge(s_y, t + 1)
                dve.wait_ge(s_hsb, t + 1)
                V.tensor_tensor(h2[:, t, :], ps_o[:, 0:P], h_sb[:, t, :], ALU.add).then_inc(s_h2, 1)
                dve.wait_ge(s_h2, t + 1)
                norm_stats(n, h2[:, t, :])
                dve.wait_ge(s_rstd, n + 1)
                V.tensor_scalar(xn2[:, t, :], h2[:, t, :], mv[:, n, 0:1], rstd[:, n:n + 1],
                                ALU.subtract, ALU.mult).then_inc(s_xn2, 1)

            def pick(src, n, k, first8):
                here = left[:, 0:n]
                for r in range(k // 8):
                    at = first8 if r == 0 else v8[:, :]
                    ins = V.max(out=at, in_=src if r == 0 else here)
                    link(ins)
                    link(V.match_replace(out=here, in_to_replace=at, in_values=src if r == 0 else here,
                                         imm_value=LOW))
                return here

            for t in range(TILES):
                dve.wait_ge(s_g1, t + 1)
                here = pick(g1[:, t, :], N_IN, K_IN, v8[:, :])
                V.scalar_tensor_tensor(out=r1[:, t, :], in0=here, scalar=PICKED, in1=g1[:, t, :], op0=ALU.is_le,
                                       op1=ALU.mult).then_inc(s_r1, 1)
                dve.wait_ge(s_r1, t + 1)
            for t in range(TILES):
                dve.wait_ge(s_g2, t + 1)
                V.max(out=top1[:, t, :], in_=g2[:, t, :]).then_inc(s_max, 1)
            for t in range(TILES):
                here = pick(g2[:, t, :], N_PROC, K_PROC, v8[:, :])
                dve.wait_ge(s_e2, t + 1)
                V.scalar_tensor_tensor(out=p2[:, t, :], in0=here, scalar=PICKED, in1=e2[:, t, :], op0=ALU.is_le,
                                       op1=ALU.mult, accum_out=psum_p[:, t:t + 1]).then_inc(s_p2, 1)
                dve.wait_ge(s_p2, t + 1)
                V.reciprocal(rsum[:, t:t + 1], psum_p[:, t:t + 1]).then_inc(s_rsum, 1)
            for t in range(TILES):
                dve.wait_ge(s_g3, t + 1)
                here = pick(g3[:, t, :], N_OUT, K_OUT, v8[:, :])
                V.scalar_tensor_tensor(out=r1[:, t, :], in0=here, scalar=PICKED, in1=g3[:, t, :], op0=ALU.is_le,
                                       op1=ALU.mult).then_inc(s_r3, 1)
                dve.wait_ge(s_r3, t + 1)
            for t in range(TILES):
                dve.wait_ge(s_o, t + 1)
                V.tensor_tensor(o_sb[:, t, :], (ps_o if t % 2 == 0 else ps_y)[:, 0:P], h2[:, t, :], ALU.add).then_inc(s_osb, 1)

        @block.tensor
        def _(pe):
            T = nc.tensor
            pe.wait_ge(s_w, 32)
            pe.wait_ge(s_const, 1)
            for t in range(TILES):
                pe.wait_ge(s_x[t], 16)
                if t >= 2:
                    pe.wait_ge(s_hsb, t - 1)
                for c in range(KC):
                    T.matmul(ps_q[t % 2][:, 0:P], xt[:, t, c, :], wt[:, c, :], start=(c == 0), stop=False)
                T.matmul(ps_q[t % 2][:, 0:P], ones[:, :], brow[:, :], start=False, stop=True).then_inc(s_h, 1)
            pe.wait_ge(s_id, 1)
            for t in range(TILES):
                pe.wait_ge(s_xn, t + 1)
                if t >= 2:
                    pe.wait_ge(s_xnt, t - 1)
                T.transpose(ps_t[t % 2][:, 0, :], xn[:, t, :], ident[:, :]).then_inc(s_tp, 1)
                pe.wait_ge(s_xnt, t + 1)
                pe.wait_ge(s_diag, TAPS)
                src = xnt[:, t, :].rearrange("p (b n) -> p b n", b=IMGS)
                dst = ps_y[:, 0:P].rearrange("p (b n) -> p b n", b=IMGS)
                if t:
                    pe.wait_ge(s_ytsb, t)
                for k in range(TAPS):
                    last = T.matmul(dst[:, :, k:], tap_diag[:, k, :], src[:, :, 0:PATCHES - k],
                                    start=(k == 0), stop=(k == TAPS - 1))
                last.then_inc(s_yt, 1)
                pe.wait_ge(s_ytsb, t + 1)
                if t:
                    pe.wait_ge(s_h2, t)
                T.matmul(ps_o[:, 0:P], yt[:, t, :], ident[:, :], start=True, stop=True).then_inc(s_y, 1)
            pe.wait_ge(s_ip, 16)
            for t in range(TILES):
                pe.wait_ge(s_xn2, t + 1)
                pe.wait_ge(s_xnt, TILES)
                if t >= 2:
                    pe.wait_ge(s_xn2t, t - 1)
                T.transpose(ps_t[t % 2][:, 0, :], xn2[:, t, :], ident[:, :]).then_inc(s_tp, 1)
                pe.wait_ge(s_xn2t, t + 1)
                if t >= 2:
                    pe.wait_ge(s_g1, t - 1)
                T.matmul(ps_z[t % 2][:, :], xn2t[:, t, :], ipt[:, :], start=True, stop=True).then_inc(s_z1, 1)
            pe.wait_ge(s_piw, 16)
            for t in range(TILES):
                pe.wait_ge(s_r1, t + 1)
                pe.wait_ge(s_xn2t, TILES)
                if t >= 2:
                    pe.wait_ge(s_rt, t - 1)
                for c in range(N_IN // P):
                    last = T.transpose(ps_t[t % 2][:, c, :], r1[:, t, c * P:(c + 1) * P], ident[:, :])
                last.then_inc(s_tp, 1)
                pe.wait_ge(s_rt, t + 1)
                pe.wait_ge(s_hsb, TILES)
                if t >= 2:
                    pe.wait_ge(s_g2, t - 1)
                for c in range(N_IN // P):
                    last = T.matmul(ps_q[t % 2][:, 0:N_PROC], rt[:, t % 2, c * P:(c + 1) * P], piwt[:, c, :],
                                    start=(c == 0), stop=(c == N_IN // P - 1))
                last.then_inc(s_z2, 1)
            pe.wait_ge(s_pv, 16)
            pe.wait_ge(s_oiw, 16)
            for t in range(TILES):
                pe.wait_ge(s_p2, t + 1)
                pe.wait_ge(s_rt, TILES + max(t - 1, 0))
                for c in range(N_PROC // P):
                    last = T.transpose(ps_t[t % 2][:, c, :], p2[:, t, c * P:(c + 1) * P], ident[:, :])
                last.then_inc(s_tp, 1)
                pe.wait_ge(s_rt, TILES + t + 1)
                if t:
                    pe.wait_ge(s_aggt, t)
                for c in range(N_PROC // P):
                    last = T.matmul(ps_y[0:D_PV, 0:P], pvs[:, c, :], rt[:, t % 2, c * P:(c + 1) * P],
                                    start=(c == 0), stop=(c == N_PROC // P - 1))
                last.then_inc(s_agg, 1)
                pe.wait_ge(s_aggt, t + 1)
                pe.wait_ge(s_g1, TILES)
                if t >= 2:
                    pe.wait_ge(s_g3, t - 1)
                T.matmul(ps_z[t % 2][:, :], aggt[:, t, :], oiwt[:, :], start=True, stop=True).then_inc(s_z3, 1)
            pe.wait_ge(s_op, 16)
            pe.wait_ge(s_h2, TILES)
            for t in range(TILES):
                pe.wait_ge(s_r3, t + 1)
                pe.wait_ge(s_rt, 2 * TILES + max(t - 1, 0))
                for c in range(N_OUT // P):
                    last = T.transpose(ps_t[t % 2][:, c, :], r1[:, t, c * P:(c + 1) * P], ident[:, :])
                last.then_inc(s_tp, 1)
                pe.wait_ge(s_rt, 2 * TILES + t + 1)
                if t >= 2:
                    pe.wait_ge(s_osb, t - 1)
                for c in range(N_OUT // P):
                    last = T.matmul((ps_o if t % 2 == 0 else ps_y)[:, 0:P], rt[:, t % 2, c * P:(c + 1) * P], ops[:, c, :],
                                    start=(c == 0), stop=(c == N_OUT // P - 1))
                last.then_inc(s_o, 1)


def kernel(**inputs):
    import numpy as np
    import concourse.bacc as bacc
    from concourse.bass_utils import run_bass_kernel_spmd

    a = {k: np.asarray(v) for k, v in inputs.items()}
    xp = a["x"].reshape(BATCH, 3, 4, 16, 4, 16).transpose(1, 3, 5, 0, 2, 4).reshape(KC, P, TILES, P)
    arrays = {
        "x_t": xp.transpose(2, 1, 0, 3),
        "w_t": a["L0_tok_W"].T.reshape(KC, P, P).transpose(1, 0, 2),
        "tok_b": a["L0_tok_b"].reshape(1, P),
        "ssm": np.concatenate([a["L0_attn_L_param"], a["L0_attn_P_left"].transpose(0, 2, 1).reshape(P, -1),
                               a["L0_attn_P_right"].reshape(P, -1), a["L0_attn_B"], a["L0_attn_C"],
                               a["L0_attn_D"].reshape(P, 1), a["L0_attn_log_dt"]], axis=1),
        "ip_t": a["L0_ffn_input_patterns"].T,
        "piw_t": a["L0_ffn_process_input_weights"].T.reshape(N_IN // P, P, N_PROC).transpose(1, 0, 2),
        "pv": a["L0_ffn_process_values"].reshape(N_PROC // P, P, D_PV).transpose(1, 0, 2),
        "oiw_t": a["L0_ffn_output_input_weights"].T,
        "op": a["L0_ffn_output_patterns"].reshape(N_OUT // P, P, P).transpose(1, 0, 2),
    }
    arrays = {k: np.ascontiguousarray(v) for k, v in arrays.items()}
    nc = bacc.Bacc("TRN2", target_bir_lowering=False, num_devices=1)
    aps = [nc.dram_tensor(k, v.shape, mybir.dt.from_np(v.dtype), kind="ExternalInput").ap()
           for k, v in arrays.items()]
    out = nc.dram_tensor("out", (TILES, P, P), FP32, kind="ExternalOutput").ap()
    build(nc, *aps, out)
    r = run_bass_kernel_spmd(nc, [arrays], core_ids=[0])
    return r.results[0]["out"].reshape(BATCH, PATCHES, P)
```

```python
import concourse.bass as bass
from concourse import mybir
from contextlib import ExitStack

FP32 = mybir.dt.float32
ALU = mybir.AluOpType
ACT = mybir.ActivationFunctionType
AX = mybir.AxisListType

P = 128
BATCH = 32
PATCHES = 16
TOK = BATCH * PATCHES
TILES = TOK // P
IMGS = P // PATCHES
KC = 6
STATE = 64
TAPS = PATCHES
N_IN, N_PROC, N_OUT, D_PV = 512, 256, 512, 64
K_IN, K_PROC, K_OUT = 64, 128, 64
EPS = 1e-5
GAUSS_MEAN = 0.3989
DENSITY_OUT = 0.2059
AIM_OUT, AIM_PROC = 57, 121
START_OUT = (2.95, 3.1)
STEPS_OUT = (1.0, 0.8, 0.6)
STEPS_PROC = (0.9, 0.8)
TINY = 1e-30
PARTS_OUT, PARTS_PROC = 4, 2
RANKS = 16
LOW = -3.0e38
PICKED = -1.0e38
C_L, C_PL, C_PR, C_B, C_C = 0, STATE, 3 * STATE, 5 * STATE, 6 * STATE
C_D, C_DT = 7 * STATE, 7 * STATE + 1
C_TB = C_DT + 1
SSM_COLS = 7 * STATE + 3
LN1_AT, XNT_AT = 3, 3


class Layer:

    def __init__(self, sem, run):
        self.picked_in = sem(f"{run}_picked_in")
        self.picked_in_t = sem(f"{run}_picked_in_t")
        self.in_t = sem(f"{run}_in_t")
        self.z_proc = sem(f"{run}_z_proc")
        self.a_proc = sem(f"{run}_a_proc")
        self.top_proc = sem(f"{run}_top_proc")
        self.neg_max = sem(f"{run}_neg_max")
        self.exp_proc = sem(f"{run}_exp_proc")
        self.weights = sem(f"{run}_weights")
        self.inv_sum = sem(f"{run}_inv_sum")
        self.weights_t = sem(f"{run}_weights_t")
        self.w_t = sem(f"{run}_w_t")
        self.agg = sem(f"{run}_agg")
        self.agg_sb = sem(f"{run}_agg_sb")
        self.z_out = sem(f"{run}_z_out")
        self.a_out = sem(f"{run}_a_out")
        self.picked_out = sem(f"{run}_picked_out")
        self.picked_out_t = sem(f"{run}_picked_out_t")
        self.out_t = sem(f"{run}_out_t")
        self.y = sem(f"{run}_y")
        self.result = sem(f"{run}_result")
        self.stored = sem(f"{run}_stored")


def build(nc, x_t, w_t, ssm, ip_t, piw_t, pv, oiw_t, op, out):
    ctx = ExitStack()
    with ctx:
        def sb(name, shape, dtype=FP32):
            return ctx.enter_context(nc.sbuf_tensor(name, shape, dtype))

        def pb(name, shape):
            return ctx.enter_context(nc.psum_tensor(name, shape, FP32))

        def sem(name):
            return ctx.enter_context(nc.semaphore(name))

        xt = sb("xt", [P, KC, TOK])
        wt = sb("wt", [P, KC, P])
        par = sb("par", [P, SSM_COLS])
        ipt = sb("ipt", [P, N_IN])
        piwt = sb("piwt", [P, N_IN // P, N_PROC])
        pvs = sb("pvs", [P, N_PROC // P, D_PV])
        oiwt = sb("oiwt", [D_PV, N_OUT])
        ops = sb("ops", [P, N_OUT // P, P])
        ident = sb("ident", [P, P])
        iota = sb("iota", [P, RANKS])
        minus_half = sb("minus_half", [P, 1])
        tiny = sb("tiny", [P, 1])
        ones_col = sb("ones_col", [P, 1])
        el = sb("el", [P, STATE])
        dt = sb("dt", [P, 1])
        hdt = sb("hdt", [P, 1])
        g = sb("g", [P, STATE])
        g_plus = sb("g_plus", [P, STATE])
        g_minus = sb("g_minus", [P, STATE])
        ig = sb("ig", [P, STATE])
        a_diag = sb("a_diag", [P, STATE])
        xu = sb("xu", [P, 2, STATE])
        yv = sb("yv", [P, 2, STATE])
        vx = sb("vx", [P, 4])
        one_minus = sb("one_minus", [P, 4])
        det = sb("det", [P, 4])
        xs = sb("xs", [P, 4, STATE])
        xh = sb("xh", [P, 2, STATE])
        xf = sb("xf", [P, 2, STATE])
        bi = sb("bi", [P, STATE])
        junk = sb("junk", [P, 6, STATE])
        wdot = sb("wdot", [P, 2])
        decayed = sb("decayed", [P, STATE])
        half_step = sb("half_step", [P, STATE])
        states = sb("states", [P, TAPS, STATE])
        cs = sb("cs", [P, TAPS, STATE])
        csum = sb("csum", [P, STATE])
        taps = sb("taps", [P, TAPS])
        tap0 = sb("tap0", [P, 1])
        tap_diag = sb("tap_diag", [P, TAPS, P])
        h_t = sb("h_t", [P, TOK])
        stats = sb("stats", [P, 2 * TILES, 6])
        mv = sb("mv", [P, 2 * TILES, 2])
        vare = sb("vare", [P, 2 * TILES])
        rstd = sb("rstd", [P, 2 * TILES])
        xn = sb("xn", [P, TILES, P])
        xn_t = sb("xn_t", [P, TOK])
        h2_t = sb("h2_t", [P, TOK])
        xn2 = sb("xn2", [P, TILES, P])
        xn2_t = sb("xn2_t", [P, TOK])
        g1 = sb("g1", [P, TILES, N_IN])
        g2 = sb("g2", [P, TILES, N_PROC])
        g3 = sb("g3", [P, TILES, N_OUT])
        e2 = sb("e2", [P, TILES, N_PROC])
        r1 = sb("r1", [P, TILES, N_IN])
        rt = sb("rt", [P, 2, N_IN])
        rt3 = sb("rt3", [P, N_OUT // P, TOK])
        p2 = sb("p2", [P, TILES, N_PROC])
        top8 = sb("top8", [P, TILES, 8])
        neg_max = sb("neg_max", [P, TILES])
        sum_p = sb("sum_p", [P, TILES])
        inv_sum = sb("inv_sum", [P, TILES])
        agg_t = sb("agg_t", [D_PV, TILES, P])
        o_sb = sb("o_sb", [P, TOK])
        gsum = sb("gsum", [P, 3 * TILES])
        guess = sb("guess", [P, 3 * TILES, 4])
        corr = sb("corr", [P, 3 * TILES, 3])
        signed = sb("signed", [P, 3 * TILES, 4])
        sign_out = sb("sign_out", [P, 2, N_IN])
        below = sb("below", [P, TILES, N_IN])
        cand = sb("cand", [P, TILES, 8 * PARTS_OUT])
        cand2 = sb("cand2", [P, TILES, 8 * PARTS_OUT])
        ranked = sb("ranked", [P, 3 * TILES, 1 + RANKS])
        last8 = sb("last8", [P, 3 * TILES])
        rank = sb("rank", [P, 3 * TILES])
        thr = sb("thr", [P, 3 * TILES])
        after = sb("after", [P, 3 * TILES])
        pick_a = sb("pick_a", [P, TILES, RANKS])
        pick_b = sb("pick_b", [P, TILES, RANKS])
        above2 = sb("above2", [P, TILES, N_PROC])
        equal2 = sb("equal2", [P, TILES, N_PROC])
        order2 = sb("order2", [P, TILES, N_PROC])
        tied2 = sb("tied2", [P, TILES, N_PROC])
        mask2 = sb("mask2", [P, TILES, N_PROC])
        n_above2 = sb("n_above2", [P, TILES])
        proofs = sb("proofs", [P, 8, TILES])
        good = sb("good", [P, 1])
        bad = sb("bad", [P, 1])
        redo = sb("redo", [1, 1], mybir.dt.int32)
        left = sb("left", [P, N_IN])
        v8 = sb("v8", [P, 8])

        ps_h = pb("ps_h", [P, TOK])
        ps_c = pb("ps_c", [P, TOK])
        ps_t = [pb(f"ps_t{i}", [P, 4, P]) for i in range(2)]
        ps_z = [pb(f"ps_z{i}", [P, N_IN]) for i in range(2)]
        ps_q = [pb(f"ps_q{i}", [P, 2 * N_PROC]) for i in range(2)]

        ps_a = [ps_h, ps_c]

        s_par, s_w = sem("s_par"), sem("s_w")
        s_x = [sem(f"s_x{c}") for c in range(KC)]
        s_ip, s_piw, s_pv, s_oiw, s_op = (sem(n) for n in ("s_ip", "s_piw", "s_pv", "s_oiw", "s_op"))
        s_zeroed, s_const = sem("s_zeroed"), sem("s_const")
        s_exp = sem("s_exp")
        s_dve = sem("s_dve")
        s_pool = sem("s_pool")
        s_state = sem("s_state")
        s_cs = sem("s_cs")
        s_tap = sem("s_tap")
        s_diag = sem("s_diag")
        s_h = sem("s_h")
        s_ht = sem("s_ht")
        s_htok = sem("s_htok")
        s_var, s_rstd = sem("s_var"), sem("s_rstd")
        s_xn, s_xnp, s_xnt = sem("s_xn"), sem("s_xnp"), sem("s_xnt")
        s_conv = sem("s_conv")
        s_h2 = sem("s_h2")
        s_h2tok = sem("s_h2tok")
        s_xn2, s_xn2p, s_xn2t = sem("s_xn2"), sem("s_xn2p"), sem("s_xn2t")
        s_z1, s_g1 = sem("s_z1"), sem("s_g1")
        s_guess = [[sem(f"s_guess{s}{n}") for n in range(4)] for s in range(3)]
        s_corr = [[sem(f"s_corr{s}{n}") for n in range(4)] for s in range(3)]
        s_count = [[sem(f"s_count{s}{n}") for n in range(4)] for s in range(3)]
        s_bad = sem("s_bad")
        s_nbad = sem("s_nbad")
        s_redo = sem("s_redo")
        fast, general = Layer(sem, "fast"), Layer(sem, "general")

        STEPS = (STEPS_OUT, STEPS_PROC, STEPS_OUT)
        WIDTH = (N_IN, N_PROC, N_OUT)
        PAIRS = ((0, 1), (2, 3))

        block = ctx.enter_context(nc.Block())

        @block.sync
        def _(sp):
            sp.dma_start(par[:, :], ssm).then_inc(s_par, 16)
            for c in range(KC):
                sp.dma_start(xt[:, c, :], x_t[c]).then_inc(s_x[c], 16)
            sp.dma_start(ipt[:, :], ip_t).then_inc(s_ip, 16)
            sp.dma_start(piwt[:, :, :], piw_t).then_inc(s_piw, 16)
            sp.dma_start(pvs[:, :, :], pv).then_inc(s_pv, 16)
            sp.dma_start(oiwt[:, :], oiw_t).then_inc(s_oiw, 16)
            sp.dma_start(ops[:, :, :], op).then_inc(s_op, 16)

            def store(run):
                for n in range(2):
                    sp.wait_ge(run.result, n + 1)
                    sp.dma_start(out[:, n * 2 * P:(n + 1) * 2 * P],
                                 o_sb[:, n * 2 * P:(n + 1) * 2 * P]).then_inc(run.stored, 16)
                sp.wait_ge(run.stored, 32)

            store(fast)
            sp.wait_ge(s_redo, 1)
            with sp.If(sp.value_load(redo[0:1, 0:1]) != 0):
                store(general)

        @block.gpsimd
        def _(pool):
            G = nc.gpsimd
            G.memset(ident[:, :], 0.0).then_inc(s_zeroed, 1)
            G.memset(minus_half[:, :], -0.5).then_inc(s_const, 1)
            G.memset(tiny[:, :], TINY).then_inc(s_const, 1)
            G.memset(ones_col[:, :], 1.0).then_inc(s_const, 1)
            G.iota(iota[:, :], pattern=[[1, RANKS]], base=0, channel_multiplier=0,
                   allow_small_or_imprecise_dtypes=True).then_inc(s_const, 1)
            pool.wait_ge(s_zeroed, 1)
            G.affine_select(out=ident[:, :], in_=ident[:, :], compare_op=ALU.not_equal, fill=1.0,
                            base=0, pattern=[[-1, P]], channel_multiplier=1).then_inc(s_const, 1)
            pool.wait_ge(s_const, 5)

            def inv_std(n):
                pool.wait_ge(s_var, n + 1)
                G.tensor_tensor(rstd[:, n:n + 1], vare[:, n:n + 1], minus_half[:, 0:1],
                                ALU.pow).then_inc(s_rstd, 1)

            pool.wait_ge(s_par, 16)
            for k in range(TAPS):
                pool.wait_ge(s_state, k + 1)
                G.tensor_tensor(cs[:, k, :], par[:, C_C:C_C + STATE], states[:, k, :], ALU.mult).then_inc(s_cs, 1)
                if k == LN1_AT:
                    for t in range(TILES):
                        inv_std(t)
            for t in range(TILES):
                inv_std(TILES + t)

            def correct(s, n, t):
                j = s * TILES + t
                width, density, aim = WIDTH[s], (0.3989 if s == 1 else DENSITY_OUT), (AIM_PROC if s == 1 else AIM_OUT)
                rate = STEPS[s][n] / (2.0 * width * GAUSS_MEAN * width * density)
                pool.wait_ge(s_count[s][n], t + 1)
                G.tensor_scalar(corr[:, j, n:n + 1], signed[:, j, n:n + 1], -rate, (width - 2 * aim) * rate,
                                ALU.mult, ALU.add).then_inc(s_corr[s][n], 1)
                old = tiny[:, 0:1] if s == 1 and n == 0 else guess[:, j, n:n + 1]
                pool.wait_ge(s_corr[s][n], t + 1)
                G.tensor_scalar(guess[:, j, n + 1:n + 2], corr[:, j, n:n + 1], gsum[:, j:j + 1], old,
                                ALU.mult, ALU.add).then_inc(s_guess[s][n + 1], 1)
                if s == 1:
                    pool.wait_ge(s_guess[s][n + 1], 2 * t + 1)
                    G.tensor_scalar(guess[:, j, n + 1:n + 2], guess[:, j, n + 1:n + 2], TINY, None,
                                    ALU.max).then_inc(s_guess[s][n + 1], 1)

            for s, a_done in enumerate((s_g1, fast.a_proc, fast.a_out)):
                for pair in PAIRS:
                    if s != 1:
                        for t in pair:
                            pool.wait_ge(a_done, t + 1)
                            j = s * TILES + t
                            G.tensor_scalar(guess[:, j, 0:1], gsum[:, j:j + 1], START_OUT[s // 2] / WIDTH[s], 0.0,
                                            ALU.mult, ALU.add).then_inc(s_guess[s][0], 1)
                    for n in range(len(STEPS[s])):
                        for t in pair:
                            correct(s, n, t)

        @block.scalar
        def _(act):
            A = nc.scalar
            act.dma_start(wt[:, :, :], w_t).then_inc(s_w, 16)
            act.wait_ge(s_par, 16)
            A.activation(el[:, :], par[:, C_L:C_L + STATE], ACT.Exp).then_inc(s_exp, 1)
            A.activation(dt[:, :], par[:, C_DT:C_DT + 1], ACT.Exp).then_inc(s_exp, 1)

            def tap(k):
                act.wait_ge(s_cs, k + 1)
                A.activation(csum[:, :], cs[:, k, :], ACT.Identity, accum_out=taps[:, k:k + 1]).then_inc(s_tap, 1)
                value = taps[:, k:k + 1]
                if k == 0:
                    act.wait_ge(s_tap, 1)
                    A.activation(tap0[:, :], taps[:, 0:1], ACT.Identity,
                                 bias=par[:, C_D:C_D + 1]).then_inc(s_tap, 1)
                    value = tap0[:, :]
                act.wait_ge(s_tap, k + 2)
                A.activation(tap_diag[:, k, :], ident[:, :], ACT.Copy, scale=value).then_inc(s_diag, 1)

            act.wait_ge(s_const, 5)
            act.wait_ge(s_h, 1)
            A.activation(h_t[:, :], ps_h[:, :], ACT.Identity, bias=par[:, C_TB:C_TB + 1]).then_inc(s_ht, 1)
            for k in range(TAPS):
                tap(k)
                if k == XNT_AT:
                    act.wait_ge(s_xnp, TILES)
                    A.activation(xn_t[:, :], ps_t[1][:, :, :], ACT.Copy).then_inc(s_xnt, 1)
            for n, pair in enumerate(PAIRS):
                act.wait_ge(s_xn2p, 2 * n + 2)
                A.activation(xn2_t[:, n * 2 * P:(n + 1) * 2 * P], ps_q[n][:, 0:2 * P], ACT.Copy).then_inc(s_xn2t, 1)

            def count(s, n, t, src):
                j = s * TILES + t
                if s == 1 and n == 0:
                    at = tiny[:, 0:1]
                else:
                    act.wait_ge(s_guess[s][n], 2 * (t + 1) if s == 1 else t + 1)
                    at = guess[:, j, n:n + 1]
                if n == 0 and t >= 2:
                    act.wait_ge(s_count[s][len(STEPS[s])], t - 1)
                elif n == 0 and s:
                    act.wait_ge(s_count[s - 1][len(STEPS[s - 1])], TILES - 1 + t)
                A.activation(sign_out[:, t % 2, 0:WIDTH[s]], src[:, t, :], ACT.Sign, scale=-1.0, bias=at,
                             accum_out=signed[:, j, n:n + 1]).then_inc(s_count[s][n], 1)

            for pair in PAIRS:
                for t in pair:
                    act.wait_ge(s_z1, t + 1)
                    A.activation(g1[:, t, :], ps_z[t % 2][:, :], ACT.Gelu, accum_out=gsum[:, t:t + 1]).then_inc(s_g1, 1)
                for n in range(len(STEPS_OUT) + 1):
                    for t in pair:
                        if n == 0:
                            act.wait_ge(s_g1, t + 1)
                        count(0, n, t, g1)

            def move_in(run, t):
                act.wait_ge(run.picked_in_t, t + 1)
                A.activation(rt[:, t % 2, :], ps_t[t % 2][:, :, :], ACT.Copy).then_inc(run.in_t, 1)

            def gelu_proc(run, t):
                act.wait_ge(run.z_proc, t + 1)
                j = TILES + t
                A.activation(g2[:, t, :], ps_q[t % 2][:, 0:N_PROC], ACT.Gelu,
                             accum_out=gsum[:, j:j + 1]).then_inc(run.a_proc, 1)

            def exp_proc(run, t):
                act.wait_ge(run.top_proc, t + 1)
                A.mul(neg_max[:, t:t + 1], top8[:, t, 0:1], -1.0).then_inc(run.neg_max, 1)
                act.wait_ge(run.neg_max, t + 1)
                A.activation(e2[:, t, :], g2[:, t, :], ACT.Exp, bias=neg_max[:, t:t + 1]).then_inc(run.exp_proc, 1)

            def move_weights(run, t):
                act.wait_ge(run.weights_t, t + 1)
                A.activation(rt[:, t % 2, 0:N_PROC], ps_t[t % 2][:, 0:2, :], ACT.Copy).then_inc(run.w_t, 1)

            def move_agg(run, t):
                act.wait_ge(run.agg, t + 1)
                A.activation(agg_t[:, t, :], ps_a[t % 2][0:D_PV, 0:P], ACT.Copy).then_inc(run.agg_sb, 1)

            def gelu_out(run, t):
                act.wait_ge(run.z_out, t + 1)
                act.wait_ge(run.inv_sum, t + 1)
                j = 2 * TILES + t
                A.activation(g3[:, t, :], ps_z[t % 2][:, :], ACT.Gelu, scale=inv_sum[:, t:t + 1],
                             accum_out=gsum[:, j:j + 1]).then_inc(run.a_out, 1)

            def move_out(run, t):
                act.wait_ge(run.picked_out_t, t + 1)
                A.activation(rt3[:, :, t * P:(t + 1) * P], ps_t[t % 2][:, :, :], ACT.Copy).then_inc(run.out_t, 1)

            for pair in PAIRS:
                for t in pair:
                    move_in(fast, t)
                for t in pair:
                    gelu_proc(fast, t)
                for n in range(len(STEPS_PROC) + 1):
                    for t in pair:
                        if n == 0:
                            act.wait_ge(fast.a_proc, t + 1)
                        count(1, n, t, g2)
                for t in pair:
                    exp_proc(fast, t)
            for pair in PAIRS:
                for t in pair:
                    move_weights(fast, t)
                for t in pair:
                    move_agg(fast, t)
                for t in pair:
                    gelu_out(fast, t)
                for n in range(len(STEPS_OUT) + 1):
                    for t in pair:
                        if n == 0:
                            act.wait_ge(fast.a_out, t + 1)
                        count(2, n, t, g3)
            for t in range(TILES):
                move_out(fast, t)

            act.wait_ge(s_redo, 1)
            with act.If(act.value_load(redo[0:1, 0:1]) != 0):
                for pair in PAIRS:
                    for t in pair:
                        move_in(general, t)
                    for t in pair:
                        gelu_proc(general, t)
                for t in range(TILES):
                    exp_proc(general, t)
                for pair in PAIRS:
                    for t in pair:
                        move_weights(general, t)
                    for t in pair:
                        move_agg(general, t)
                    for t in pair:
                        gelu_out(general, t)
                for t in range(TILES):
                    move_out(general, t)

        @block.vector
        def _(dve):
            V = nc.vector
            steps = [0]

            def step(ins):
                ins.then_inc(s_dve, 1)
                steps[0] += 1
                return steps[0]

            def after_step(n):
                dve.wait_ge(s_dve, n)

            vr = par[:, C_PR:C_PR + 2 * STATE].rearrange("p (i n) -> p i n", i=2)
            pl = par[:, C_PL:C_PL + 2 * STATE].rearrange("p (i n) -> p i n", i=2)

            def dot(out_, u, v, j):
                return V.scalar_tensor_tensor(out=junk[:, j, :], in0=u, scalar=1.0, in1=v, op0=ALU.mult,
                                              op1=ALU.mult, accum_out=out_)

            dve.wait_ge(s_par, 16)
            dve.wait_ge(s_exp, 2)
            n = step(V.tensor_scalar(hdt[:, :], dt[:, :], 0.5, None, ALU.mult))
            after_step(n)
            n = step(V.tensor_scalar(g[:, :], el[:, :], hdt[:, 0:1], None, ALU.mult))
            after_step(n)
            n = step(V.tensor_scalar(g_plus[:, :], g[:, :], 1.0, None, ALU.add))
            step(V.tensor_scalar(g_minus[:, :], g[:, :], -1.0, 1.0, ALU.mult, ALU.add))
            after_step(n)
            n = step(V.reciprocal(ig[:, :], g_plus[:, :]))
            after_step(n)
            for i in range(2):
                step(V.scalar_tensor_tensor(out=xu[:, i, :], in0=pl[:, i, :], scalar=hdt[:, 0:1], in1=ig[:, :],
                                            op0=ALU.mult, op1=ALU.mult))
            step(V.scalar_tensor_tensor(out=bi[:, :], in0=par[:, C_B:C_B + STATE], scalar=dt[:, 0:1],
                                        in1=ig[:, :], op0=ALU.mult, op1=ALU.mult))
            for i in range(2):
                n = step(V.tensor_tensor(yv[:, i, :], vr[:, i, :], ig[:, :], ALU.mult))
            step(V.tensor_tensor(a_diag[:, :], g_minus[:, :], ig[:, :], ALU.mult))
            after_step(n)
            for i in range(2):
                for j in range(2):
                    n = step(dot(vx[:, 2 * i + j:2 * i + j + 1], vr[:, i, :], xu[:, j, :], 2 * i + j))
            for i in range(2):
                step(dot(wdot[:, i:i + 1], vr[:, i, :], bi[:, :], 4 + i))
            after_step(n)
            n = step(V.tensor_scalar(one_minus[:, :], vx[:, :], -1.0, 1.0, ALU.mult, ALU.add))
            step(V.tensor_tensor(det[:, 1:2], vx[:, 1:2], vx[:, 2:3], ALU.mult))
            after_step(n)
            n = step(V.tensor_tensor(det[:, 0:1], one_minus[:, 0:1], one_minus[:, 3:4], ALU.mult))
            after_step(n)
            n = step(V.tensor_tensor(det[:, 2:3], det[:, 0:1], det[:, 1:2], ALU.subtract))
            after_step(n)
            n = step(V.reciprocal(det[:, 3:4], det[:, 2:3]))
            after_step(n)
            column = ((one_minus[:, 3:4], vx[:, 2:3]), (vx[:, 1:2], one_minus[:, 0:1]))
            for j in range(2):
                for i in range(2):
                    n = step(V.tensor_scalar(xs[:, 2 * j + i, :], xu[:, i, :], column[j][i], det[:, 3:4],
                                             ALU.mult, ALU.mult))
            after_step(n)
            for j in range(2):
                n = step(V.tensor_tensor(xh[:, j, :], xs[:, 2 * j, :], xs[:, 2 * j + 1, :], ALU.add))
            after_step(n)
            n = step(V.scalar_tensor_tensor(out=half_step[:, :], in0=xh[:, 0, :], scalar=wdot[:, 0:1],
                                            in1=bi[:, :], op0=ALU.mult, op1=ALU.add))
            step(V.tensor_scalar(xf[:, :, :], xh[:, :, :], 2.0, None, ALU.mult))
            after_step(n)
            V.scalar_tensor_tensor(out=states[:, 0, :], in0=xh[:, 1, :], scalar=wdot[:, 1:2],
                                   in1=half_step[:, :], op0=ALU.mult, op1=ALU.add).then_inc(s_state, 1)

            def norm_stats(first, tiles, src):
                for t in tiles:
                    n = step(V.bn_stats(out=stats[:, first + t, :], in_=src(t)))
                after_step(n)
                for t in tiles:
                    n = step(V.bn_aggr(out=mv[:, first + t, :], in_=stats[:, first + t, :]))
                for t in tiles:
                    after_step(n - len(tiles) + 1 + (t - tiles[0]))
                    V.tensor_scalar(vare[:, first + t:first + t + 1], mv[:, first + t, 1:2], EPS, None,
                                    ALU.add).then_inc(s_var, 1)

            def norm_apply(first, t, dst, src, done):
                dve.wait_ge(s_rstd, first + t + 1)
                V.tensor_scalar(dst, src, mv[:, first + t, 0:1], rstd[:, first + t:first + t + 1],
                                ALU.subtract, ALU.mult).then_inc(done, 1)

            for k in range(1, TAPS):
                dve.wait_ge(s_state, k)
                s = states[:, k - 1, :]
                step(dot(wdot[:, 0:1], yv[:, 0, :], s, 0))
                n = step(dot(wdot[:, 1:2], yv[:, 1, :], s, 1))
                m = step(V.tensor_tensor(decayed[:, :], a_diag[:, :], s, ALU.mult))
                after_step(m)
                n = step(V.scalar_tensor_tensor(out=half_step[:, :], in0=xf[:, 0, :], scalar=wdot[:, 0:1],
                                                in1=decayed[:, :], op0=ALU.mult, op1=ALU.add))
                after_step(n)
                V.scalar_tensor_tensor(out=states[:, k, :], in0=xf[:, 1, :], scalar=wdot[:, 1:2],
                                       in1=half_step[:, :], op0=ALU.mult, op1=ALU.add).then_inc(s_state, 1)
                if k == LN1_AT:
                    dve.wait_ge(s_htok, TILES)
                    norm_stats(0, range(TILES), lambda t: ps_t[0][:, t, :])
                if k == LN1_AT + 1:
                    for t in range(TILES):
                        norm_apply(0, t, xn[:, t, :], ps_t[0][:, t, :], s_xn)
            dve.wait_ge(s_conv, 1)
            for n in range(2):
                V.tensor_tensor(h2_t[:, n * 2 * P:(n + 1) * 2 * P], ps_c[:, n * 2 * P:(n + 1) * 2 * P],
                                h_t[:, n * 2 * P:(n + 1) * 2 * P], ALU.add).then_inc(s_h2, 1)
            for n, pair in enumerate(PAIRS):
                dve.wait_ge(s_h2tok, n + 1)
                norm_stats(TILES, pair, lambda t: ps_t[n][:, t % 2, :])
            for n, pair in enumerate(PAIRS):
                for t in pair:
                    norm_apply(TILES, t, xn2[:, t, :], ps_t[n][:, t % 2, :], s_xn2)

            def candidates(s, pair, src, parts):
                width, last = WIDTH[s], len(STEPS[s])
                for t in pair:
                    j = s * TILES + t
                    dve.wait_ge(s_guess[s][last], 2 * (t + 1) if s == 1 else t + 1)
                    n = step(V.scalar_tensor_tensor(out=below[:, t, 0:width], in0=src[:, t, :],
                                                    scalar=guess[:, j, last:last + 1], in1=src[:, t, :],
                                                    op0=ALU.is_le, op1=ALU.mult))
                    step(V.tensor_copy(ranked[:, j, 0:1], guess[:, j, last:last + 1]))
                for t in pair:
                    after_step(n - 2 * (pair[1] - t))
                    for q in range(parts):
                        m = step(V.max(out=cand[:, t, 8 * q:8 * q + 8],
                                       in_=below[:, t, q * width // parts:(q + 1) * width // parts]))
                ends = m
                for t in pair:
                    j = s * TILES + t
                    after_step(ends - parts * (pair[1] - t))
                    step(V.max(out=ranked[:, j, 1:9], in_=cand[:, t, 0:8 * parts]))
                    if s != 1:
                        m = step(V.tensor_reduce(out=last8[:, j:j + 1], in_=cand[:, t, 7:8 * parts:8],
                                                 axis=AX.X, op=ALU.max))
                    else:
                        m = steps[0]
                for t in pair:
                    j = s * TILES + t
                    after_step(m if t == pair[1] or s == 1 and t == pair[1] else m - (2 if s != 1 else 1))
                    n = step(V.match_replace(out=cand2[:, t, 0:8 * parts], in_to_replace=ranked[:, j, 1:9],
                                             in_values=cand[:, t, 0:8 * parts], imm_value=LOW))
                for t in pair:
                    j = s * TILES + t
                    after_step(n - (pair[1] - t))
                    m = step(V.max(out=ranked[:, j, 9:17], in_=cand2[:, t, 0:8 * parts]))

            def threshold(s, pair, k):
                for t in pair:
                    j = s * TILES + t
                    last = len(STEPS[s])
                    dve.wait_ge(s_count[s][last], t + 1)
                    n = step(V.tensor_scalar(rank[:, j:j + 1], signed[:, j, last:last + 1], 0.5,
                                             k - WIDTH[s] / 2.0, ALU.mult, ALU.add))
                for t in pair:
                    j = s * TILES + t
                    after_step(n - (pair[1] - t))
                    m = step(V.scalar_tensor_tensor(out=pick_a[:, t, :], in0=iota[:, :], scalar=rank[:, j:j + 1],
                                                    in1=ranked[:, j, 0:RANKS], op0=ALU.is_equal, op1=ALU.mult,
                                                    accum_out=thr[:, j:j + 1]))
                if s != 1:
                    for t in pair:
                        j = s * TILES + t
                        step(V.scalar_tensor_tensor(out=pick_b[:, t, :], in0=iota[:, :], scalar=rank[:, j:j + 1],
                                                    in1=ranked[:, j, 1:RANKS + 1], op0=ALU.is_equal,
                                                    op1=ALU.mult, accum_out=after[:, j:j + 1]))
                after_step(m)

            def keep_largest(s, pair, src, done):
                candidates(s, pair, src, PARTS_OUT)
                threshold(s, pair, K_IN if s == 0 else K_OUT)
                for t in pair:
                    j = s * TILES + t
                    V.scalar_tensor_tensor(out=r1[:, t, :], in0=src[:, t, :], scalar=thr[:, j:j + 1],
                                           in1=src[:, t, :], op0=ALU.is_ge, op1=ALU.mult).then_inc(done, 1)

            def finish_weights(run, t, mask, scalar, op0):
                dve.wait_ge(run.exp_proc, t + 1)
                V.scalar_tensor_tensor(out=p2[:, t, :], in0=mask, scalar=scalar, in1=e2[:, t, :],
                                       op0=op0, op1=ALU.mult, accum_out=sum_p[:, t:t + 1]).then_inc(run.weights, 1)
                dve.wait_ge(run.weights, t + 1)
                V.reciprocal(inv_sum[:, t:t + 1], sum_p[:, t:t + 1]).then_inc(run.inv_sum, 1)

            for pair in PAIRS:
                keep_largest(0, pair, g1, fast.picked_in)
            dve.wait_ge(s_const, 5)
            for pair in PAIRS:
                for t in pair:
                    dve.wait_ge(fast.a_proc, t + 1)
                    V.max(out=top8[:, t, :], in_=g2[:, t, :]).then_inc(fast.top_proc, 1)
                candidates(1, pair, g2, PARTS_PROC)
                threshold(1, pair, K_PROC)
                for t in pair:
                    j = TILES + t
                    n = step(V.tensor_scalar(equal2[:, t, :], g2[:, t, :], thr[:, j:j + 1], None, ALU.is_equal))
                    m = step(V.tensor_scalar(above2[:, t, :], g2[:, t, :], thr[:, j:j + 1], None, ALU.is_gt,
                                             ALU.add, accum_out=n_above2[:, t:t + 1]))
                for t in pair:
                    after_step(m - 2 * (pair[1] - t))
                    n = step(V.tensor_tensor_scan(order2[:, t, :], equal2[:, t, :], equal2[:, t, :],
                                                  n_above2[:, t:t + 1], ALU.add, ALU.max))
                for t in pair:
                    after_step(n - (pair[1] - t))
                    m = step(V.scalar_tensor_tensor(out=tied2[:, t, :], in0=order2[:, t, :], scalar=float(K_PROC),
                                                    in1=equal2[:, t, :], op0=ALU.is_le, op1=ALU.mult))
                for t in pair:
                    after_step(m - (pair[1] - t))
                    n = step(V.tensor_tensor(mask2[:, t, :], tied2[:, t, :], above2[:, t, :], ALU.add))
                for t in pair:
                    after_step(n - (pair[1] - t))
                    finish_weights(fast, t, mask2[:, t, :], 1.0, ALU.mult)
            for pair in PAIRS:
                keep_largest(2, pair, g3, fast.picked_out)

            def prove():
                after_step(steps[0])
                for i, s in enumerate((0, 2)):
                    rows = slice(s * TILES, (s + 1) * TILES)
                    step(V.tensor_tensor(proofs[:, 3 * i, :], ranked[:, rows, 1], ranked[:, rows, 0], ALU.is_lt))
                    step(V.tensor_tensor(proofs[:, 3 * i + 1, :], after[:, rows], thr[:, rows], ALU.is_lt))
                    step(V.tensor_tensor(proofs[:, 3 * i + 2, :], last8[:, rows], thr[:, rows], ALU.is_lt))
                step(V.tensor_scalar(proofs[:, 6, :], n_above2[:, :], float(K_PROC), None, ALU.is_le))
                n = step(V.tensor_scalar(proofs[:, 7, :], order2[:, :, N_PROC - 1], float(K_PROC), None, ALU.is_ge))
                after_step(n)
                n = step(V.tensor_reduce(out=good[:, :], in_=proofs[:, :, :], axis=AX.XY, op=ALU.min))
                after_step(n)
                V.tensor_scalar(bad[:, :], good[:, :], -1.0, 1.0, ALU.mult, ALU.add).then_inc(s_bad, 1)

            def results(run):
                for n in range(2):
                    dve.wait_ge(run.y, n + 1)
                    V.tensor_tensor(o_sb[:, n * 2 * P:(n + 1) * 2 * P], ps_a[n][:, 0:2 * P],
                                    h2_t[:, n * 2 * P:(n + 1) * 2 * P], ALU.add).then_inc(run.result, 1)

            prove()
            results(fast)
            dve.wait_ge(s_nbad, 1)
            V.tensor_copy(redo[:, :], ps_q[0][0:1, 0:1]).then_inc(s_redo, 1)

            dve.wait_ge(s_redo, 1)
            with dve.If(dve.value_load(redo[0:1, 0:1]) != 0):
                def mark_largest(src, width, k):
                    for r in range(k // 8):
                        now = src if r == 0 else left[:, 0:width]
                        n = step(V.max(out=v8[:, :], in_=now))
                        after_step(n)
                        n = step(V.match_replace(out=left[:, 0:width], in_to_replace=v8[:, :], in_values=now,
                                                 imm_value=LOW))
                        after_step(n)

                def keep_marked(src, t, done):
                    V.scalar_tensor_tensor(out=r1[:, t, :], in0=left[:, :], scalar=PICKED, in1=src[:, t, :],
                                           op0=ALU.is_le, op1=ALU.mult).then_inc(done, 1)
                    dve.wait_ge(done, t + 1)

                for t in range(TILES):
                    mark_largest(g1[:, t, :], N_IN, K_IN)
                    keep_marked(g1, t, general.picked_in)
                for t in range(TILES):
                    dve.wait_ge(general.a_proc, t + 1)
                    V.max(out=top8[:, t, :], in_=g2[:, t, :]).then_inc(general.top_proc, 1)
                for t in range(TILES):
                    mark_largest(g2[:, t, :], N_PROC, K_PROC)
                    finish_weights(general, t, left[:, 0:N_PROC], PICKED, ALU.is_le)
                for t in range(TILES):
                    dve.wait_ge(general.a_out, t + 1)
                    mark_largest(g3[:, t, :], N_OUT, K_OUT)
                    keep_marked(g3, t, general.picked_out)
                dve.wait_ge(fast.stored, 32)
                results(general)

        @block.tensor
        def _(pe):
            T = nc.tensor
            pe.wait_ge(s_w, 16)
            for c in range(KC):
                pe.wait_ge(s_x[c], 16)
                last = T.matmul(ps_h[:, :], wt[:, c, :], xt[:, c, :], start=(c == 0), stop=(c == KC - 1))
            last.then_inc(s_h, 1)
            pe.wait_ge(s_const, 5)
            pe.wait_ge(s_ht, 1)
            for t in range(TILES):
                T.transpose(ps_t[0][:, t, :], h_t[:, t * P:(t + 1) * P], ident[:, :]).then_inc(s_htok, 1)
            for t in range(TILES):
                pe.wait_ge(s_xn, t + 1)
                T.transpose(ps_t[1][:, t, :], xn[:, t, :], ident[:, :]).then_inc(s_xnp, 1)
            pe.wait_ge(s_xnt, 1)
            src = xn_t[:, :].rearrange("p (b n) -> p b n", b=BATCH)
            dst = ps_c[:, :].rearrange("p (b n) -> p b n", b=BATCH)
            for k in range(TAPS):
                pe.wait_ge(s_diag, k + 1)
                last = T.matmul(dst[:, :, k:], tap_diag[:, k, :], src[:, :, 0:PATCHES - k],
                                start=(k == 0), stop=(k == TAPS - 1))
            last.then_inc(s_conv, 1)
            for n, pair in enumerate(PAIRS):
                pe.wait_ge(s_h2, n + 1)
                for t in pair:
                    last = T.transpose(ps_t[n][:, t % 2, :], h2_t[:, t * P:(t + 1) * P], ident[:, :])
                last.then_inc(s_h2tok, 1)
            pe.wait_ge(s_ip, 16)
            for n, pair in enumerate(PAIRS):
                for t in pair:
                    pe.wait_ge(s_xn2, t + 1)
                    T.transpose(ps_q[n][:, (t % 2) * P:(t % 2 + 1) * P], xn2[:, t, :],
                                ident[:, :]).then_inc(s_xn2p, 1)
            for n, pair in enumerate(PAIRS):
                pe.wait_ge(s_xn2t, n + 1)
                for t in pair:
                    if t >= 2:
                        pe.wait_ge(s_g1, t - 1)
                    T.matmul(ps_z[t % 2][:, :], xn2_t[:, t * P:(t + 1) * P], ipt[:, :], start=True,
                             stop=True).then_inc(s_z1, 1)

            def transposes(src, t, chunks, done):
                for c in range(chunks):
                    last = T.transpose(ps_t[t % 2][:, c, :], src[:, t, c * P:(c + 1) * P], ident[:, :])
                last.then_inc(done, 1)

            def layer(run):
                pe.wait_ge(s_piw, 16)
                for pair in PAIRS:
                    for t in pair:
                        pe.wait_ge(run.picked_in, t + 1)
                        if t >= 2:
                            pe.wait_ge(run.in_t, t - 1)
                        transposes(r1, t, N_IN // P, run.picked_in_t)
                    for t in pair:
                        pe.wait_ge(run.in_t, t + 1)
                        if t >= 2:
                            pe.wait_ge(run.a_proc, t - 1)
                        for c in range(N_IN // P):
                            last = T.matmul(ps_q[t % 2][:, 0:N_PROC], rt[:, t % 2, c * P:(c + 1) * P],
                                            piwt[:, c, :], start=(c == 0), stop=(c == N_IN // P - 1))
                        last.then_inc(run.z_proc, 1)
                pe.wait_ge(s_pv, 16)
                pe.wait_ge(s_oiw, 16)
                for pair in PAIRS:
                    for t in pair:
                        pe.wait_ge(run.weights, t + 1)
                        if t >= 2:
                            pe.wait_ge(run.w_t, t - 1)
                        transposes(p2, t, N_PROC // P, run.weights_t)
                    for t in pair:
                        pe.wait_ge(run.w_t, t + 1)
                        if t >= 2:
                            pe.wait_ge(run.agg_sb, t - 1)
                        for c in range(N_PROC // P):
                            last = T.matmul(ps_a[t % 2][0:D_PV, 0:P], pvs[:, c, :],
                                            rt[:, t % 2, c * P:(c + 1) * P],
                                            start=(c == 0), stop=(c == N_PROC // P - 1))
                        last.then_inc(run.agg, 1)
                    for t in pair:
                        pe.wait_ge(run.agg_sb, t + 1)
                        if t >= 2:
                            pe.wait_ge(run.a_out, t - 1)
                        T.matmul(ps_z[t % 2][:, :], agg_t[:, t, :], oiwt[:, :], start=True,
                                 stop=True).then_inc(run.z_out, 1)
                pe.wait_ge(s_op, 16)
                for n, pair in enumerate(PAIRS):
                    for t in pair:
                        pe.wait_ge(run.picked_out, t + 1)
                        if t >= 2:
                            pe.wait_ge(run.out_t, t - 1)
                        transposes(r1, t, N_OUT // P, run.picked_out_t)
                    pe.wait_ge(run.out_t, 2 * n + 2)
                    for c in range(N_OUT // P):
                        last = T.matmul(ps_a[n][:, 0:2 * P], ops[:, c, :],
                                        rt3[:, c, n * 2 * P:(n + 1) * 2 * P],
                                        start=(c == 0), stop=(c == N_OUT // P - 1))
                    last.then_inc(run.y, 1)

            layer(fast)
            pe.wait_ge(s_bad, 1)
            T.matmul(ps_q[0][0:1, 0:1], bad[:, :], ones_col[:, :], start=True, stop=True).then_inc(s_nbad, 1)
            pe.wait_ge(s_redo, 1)
            with pe.If(pe.value_load(redo[0:1, 0:1]) != 0):
                layer(general)


def kernel(**inputs):
    import numpy as np
    import concourse.bacc as bacc
    from concourse.bass_utils import run_bass_kernel_spmd

    a = {k: np.asarray(v) for k, v in inputs.items()}
    xp = a["x"].reshape(BATCH, 3, 4, 16, 4, 16).transpose(1, 3, 5, 0, 2, 4).reshape(KC, P, TILES, P)
    arrays = {
        "x_t": xp.reshape(KC, P, TOK),
        "w_t": a["L0_tok_W"].T.reshape(KC, P, P).transpose(1, 0, 2),
        "ssm": np.concatenate([a["L0_attn_L_param"], a["L0_attn_P_left"].transpose(0, 2, 1).reshape(P, -1),
                               a["L0_attn_P_right"].reshape(P, -1), a["L0_attn_B"], a["L0_attn_C"],
                               a["L0_attn_D"].reshape(P, 1), a["L0_attn_log_dt"], a["L0_tok_b"].reshape(P, 1)], axis=1),
        "ip_t": a["L0_ffn_input_patterns"].T,
        "piw_t": a["L0_ffn_process_input_weights"].T.reshape(N_IN // P, P, N_PROC).transpose(1, 0, 2),
        "pv": a["L0_ffn_process_values"].reshape(N_PROC // P, P, D_PV).transpose(1, 0, 2),
        "oiw_t": a["L0_ffn_output_input_weights"].T,
        "op": a["L0_ffn_output_patterns"].reshape(N_OUT // P, P, P).transpose(1, 0, 2),
    }
    arrays = {k: np.ascontiguousarray(v) for k, v in arrays.items()}
    nc = bacc.Bacc("TRN2", target_bir_lowering=False, num_devices=1)
    aps = [nc.dram_tensor(k, v.shape, mybir.dt.from_np(v.dtype), kind="ExternalInput").ap()
           for k, v in arrays.items()]
    out = nc.dram_tensor("out", (P, TOK), FP32, kind="ExternalOutput").ap()
    build(nc, *aps, out)
    r = run_bass_kernel_spmd(nc, [arrays], core_ids=[0])
    return r.results[0]["out"].T.reshape(BATCH, PATCHES, P)
```

```python
import concourse.bass as bass
from concourse import mybir
from contextlib import ExitStack

FP32 = mybir.dt.float32
ALU = mybir.AluOpType
ACT = mybir.ActivationFunctionType
AX = mybir.AxisListType

P = 128
BATCH = 32
PATCHES = 16
TOK = BATCH * PATCHES
TILES = TOK // P
KC = 6
XG = 3
STATE = 64
TAPS = PATCHES
HALF = TAPS // 2
N_IN, N_PROC, N_OUT, D_PV = 512, 256, 512, 64
K_IN, K_PROC, K_OUT = 64, 128, 64
EPS = 1e-5
GAUSS_MEAN = 0.3989
DENSITY_OUT = 0.2059
AIM_OUT, AIM_PROC = 53, 114
START_OUT = (2.95, 3.1)
STEP_OUT, STEP_PROC = 0.9, 0.85
TINY = 1e-30
PARTS = 8
RANKS = (24, 32, 24)
COUNTS = (3, 2, 3)
LOW = -3.0e38
PICKED = -1.0e38
C_L, C_PL, C_PR, C_B, C_C = 0, STATE, 3 * STATE, 5 * STATE, 6 * STATE
C_D, C_DT = 7 * STATE, 7 * STATE + 1
C_TB = C_DT + 1
SSM_COLS = 7 * STATE + 3
NORM1_AT = (1, 3)
DVE_DIAG = 12
FIRST_TAPS = 4
WARM = 10
WARM_LAYER = (5, 4, 12, 6, 6, 10, 12)


class Layer:

    def __init__(self, sem, run):
        self.picked_in = sem(f"{run}_picked_in")
        self.picked_in_t = sem(f"{run}_picked_in_t")
        self.in_t = sem(f"{run}_in_t")
        self.z_proc = sem(f"{run}_z_proc")
        self.a_proc = sem(f"{run}_a_proc")
        self.top_proc = sem(f"{run}_top_proc")
        self.neg_max = sem(f"{run}_neg_max")
        self.exp_proc = sem(f"{run}_exp_proc")
        self.weights = sem(f"{run}_weights")
        self.inv_sum = sem(f"{run}_inv_sum")
        self.weights_t = sem(f"{run}_weights_t")
        self.w_t = sem(f"{run}_w_t")
        self.agg = sem(f"{run}_agg")
        self.agg_sb = sem(f"{run}_agg_sb")
        self.z_out = sem(f"{run}_z_out")
        self.a_out = sem(f"{run}_a_out")
        self.picked_out = sem(f"{run}_picked_out")
        self.picked_out_t = sem(f"{run}_picked_out_t")
        self.out_t = sem(f"{run}_out_t")
        self.y = sem(f"{run}_y")
        self.result = sem(f"{run}_result")
        self.stored = sem(f"{run}_stored")


def build(nc, x_t, w_t, ssm, ip_t, piw_t, pv, oiw_t, op, out):
    ctx = ExitStack()
    with ctx:
        def sb(name, shape, dtype=FP32):
            return ctx.enter_context(nc.sbuf_tensor(name, shape, dtype))

        def pb(name, shape):
            return ctx.enter_context(nc.psum_tensor(name, shape, FP32))

        def sem(name):
            return ctx.enter_context(nc.semaphore(name))

        xt = sb("xt", [P, 2 * XG, KC // XG, 2 * P])
        wt = sb("wt", [P, KC, P])
        par = sb("par", [P, SSM_COLS])
        ipt = sb("ipt", [P, N_IN])
        piwt = sb("piwt", [P, N_IN // P, N_PROC])
        pvs = sb("pvs", [P, N_PROC // P, D_PV])
        oiwt = sb("oiwt", [D_PV, N_OUT])
        ops = sb("ops", [P, N_OUT // P, P])
        warm = sb("warm", [P, TOK])
        ident = sb("ident", [P, P])
        centre = sb("centre", [P, P])
        iota = sb("iota", [P, max(RANKS)])
        minus_half = sb("minus_half", [P, TILES])
        tiny = sb("tiny", [P, 1])
        ones_col = sb("ones_col", [P, 1])
        el = sb("el", [P, STATE])
        dt = sb("dt", [P, 1])
        hdt = sb("hdt", [P, 1])
        g = sb("g", [P, STATE])
        g_plus = sb("g_plus", [P, STATE])
        g_minus = sb("g_minus", [P, STATE])
        ig = sb("ig", [P, STATE])
        a_diag = sb("a_diag", [P, STATE])
        xu = sb("xu", [P, 2, STATE])
        yv = sb("yv", [P, 2, STATE])
        vx = sb("vx", [P, 4])
        one_minus = sb("one_minus", [P, 4])
        det = sb("det", [P, 4])
        own = sb("own", [P, 4])
        other = sb("other", [P, 4])
        xs = sb("xs", [P, 2, STATE])
        xf = sb("xf", [P, 2, STATE])
        bi = sb("bi", [P, STATE])
        junk = sb("junk", [P, 8, STATE])
        bdot = sb("bdot", [P, 2])
        half_bdot = sb("half_bdot", [P, 2])
        wdot = sb("wdot", [P, 2])
        udot = sb("udot", [P, 2])
        decayed_x = sb("decayed_x", [P, STATE])
        decayed_y = sb("decayed_y", [P, STATE])
        half_x = sb("half_x", [P, STATE])
        half_y = sb("half_y", [P, STATE])
        states = sb("states", [P, HALF, STATE])
        adjoint = sb("adjoint", [P, 2, STATE])
        cs = sb("cs", [P, HALF, STATE])
        csum = sb("csum", [P, STATE])
        taps = sb("taps", [P, TAPS])
        tap0 = sb("tap0", [P, 1])
        tap_diag = sb("tap_diag", [P, TAPS, P])
        h_t = sb("h_t", [P, TOK])
        hsq, var1, rstd1 = (sb(name, [P, TILES]) for name in ("hsq", "var1", "rstd1"))
        stats = sb("stats", [P, TILES, 6])
        mv = sb("mv", [P, TILES, 2])
        norm_junk = sb("norm_junk", [P, TILES, P])
        gelu_junk = sb("gelu_junk", [P, 1])
        vare = sb("vare", [P, TILES])
        rstd = sb("rstd", [P, TILES])
        xn = sb("xn", [P, TILES, P])
        xn_t = sb("xn_t", [P, TOK])
        h2_t = sb("h2_t", [P, TOK])
        ipc = sb("ipc", [P, N_IN])
        g1 = sb("g1", [P, TILES, N_IN])
        g2 = sb("g2", [P, TILES, N_PROC])
        g3 = sb("g3", [P, TILES, N_OUT])
        e2 = sb("e2", [P, TILES, N_PROC])
        r1 = sb("r1", [P, TILES, N_IN])
        rt = sb("rt", [P, 2, N_IN])
        rt3 = sb("rt3", [P, N_OUT // P, TOK])
        p2 = sb("p2", [P, TILES, N_PROC])
        top8 = sb("top8", [P, TILES, 8])
        neg_max = sb("neg_max", [P, TILES])
        sum_p = sb("sum_p", [P, TILES])
        inv_sum = sb("inv_sum", [P, TILES])
        agg_t = sb("agg_t", [D_PV, TILES, P])
        o_sb = sb("o_sb", [P, TOK])
        gsum = sb("gsum", [P, 3 * TILES])
        guess = sb("guess", [P, 2, 3 * TILES])
        counted = sb("counted", [P, 3 * TILES, 3])
        slope = sb("slope", [P, 3 * TILES])
        base = sb("base", [P, 3 * TILES])
        start = sb("start", [P, 2, 3 * TILES])
        sign_out = sb("sign_out", [P, 2, N_IN])
        above_out = sb("above_out", [P, N_IN])
        off_junk = sb("off_junk", [P, N_IN])
        off_guess = sb("off_guess", [P, 1])
        below = sb("below", [P, TILES, N_IN])
        cands = [sb(f"cand{s}", [P, TILES, 8 * PARTS]) for s in range(3)]
        cand_left = [sb(f"cand_left{r}", [P, TILES, 8 * PARTS]) for r in range(max(RANKS) // 8 - 1)]
        ranked = sb("ranked", [P, 3 * TILES, 1 + max(RANKS)])
        last8 = sb("last8", [P, 3 * TILES])
        rank = sb("rank", [P, 3 * TILES])
        thr = sb("thr", [P, 3 * TILES])
        after = sb("after", [P, 3 * TILES])
        pick_a = sb("pick_a", [P, TILES, max(RANKS)])
        pick_b = sb("pick_b", [P, TILES, max(RANKS)])
        side2 = sb("side2", [P, TILES, N_PROC])
        equal2 = sb("equal2", [P, TILES, N_PROC])
        order2 = sb("order2", [P, TILES, N_PROC])
        mask2 = sb("mask2", [P, TILES, N_PROC])
        sides2 = sb("sides2", [P, TILES])
        half_sides2 = sb("half_sides2", [P, TILES])
        n_tied2 = sb("n_tied2", [P, TILES])
        proofs = sb("proofs", [P, 8, TILES])
        good = sb("good", [P, 1])
        bad = sb("bad", [P, 1])
        redo = sb("redo", [1, 1], mybir.dt.int32)
        left = sb("left", [P, N_IN])
        v8 = sb("v8", [P, 8])

        ps_h = pb("ps_h", [P, TOK])
        ps_c = pb("ps_c", [P, TOK])
        ps_t = [pb(f"ps_t{i}", [P, 4, P]) for i in range(2)]
        ps_z = [pb(f"ps_z{i}", [P, N_IN]) for i in range(2)]
        ps_q = [pb(f"ps_q{i}", [P, 2 * N_PROC]) for i in range(2)]

        ps_a = [ps_h, ps_z[1]]
        ps_norm2 = [ps_t[0][:, 0, :], ps_t[1][:, 0, :], ps_q[0], ps_q[1]]
        ps_y = [ps_c, ps_q[0]]

        s_par, s_w = sem("s_par"), sem("s_w")
        s_x = [sem(f"s_x{c}") for c in range(2 * XG)]
        s_ip, s_piw, s_pv, s_oiw, s_op = (sem(n) for n in ("s_ip", "s_piw", "s_pv", "s_oiw", "s_op"))
        s_gelu_table = sem("s_gelu_table")
        s_zeroed, s_const = sem("s_zeroed"), sem("s_const")
        s_exp = sem("s_exp")
        s_dve = sem("s_dve")
        s_pool = sem("s_pool")
        s_state = sem("s_state")
        s_adjoint = sem("s_adjoint")
        s_ig = sem("s_ig")
        s_y = sem("s_y")
        s_decayed_x = sem("s_decayed_x")
        s_decayed_y = sem("s_decayed_y")
        s_cs = sem("s_cs")
        s_tap = sem("s_tap")
        s_late_tap = sem("s_late_tap")
        s_diag = sem("s_diag")
        s_late_diag = sem("s_late_diag")
        s_opened = sem("s_opened")
        s_warm = sem("s_warm")
        s_warmed = sem("s_warmed")
        s_h = sem("s_h")
        s_ht = sem("s_ht")
        s_htok = sem("s_htok")
        s_hsq = sem("s_hsq")
        s_std1 = sem("s_std1")
        s_ipc_z = sem("s_ipc_z")
        s_ipc = sem("s_ipc")
        s_xn = sem("s_xn")
        s_xnp = sem("s_xnp")
        s_xnt = sem("s_xnt")
        s_conv = sem("s_conv")
        s_h2 = sem("s_h2")
        s_h2tok = sem("s_h2tok")
        s_var = sem("s_var")
        s_rstd = sem("s_rstd")
        s_z1 = sem("s_z1")
        s_g1 = sem("s_g1")
        s_guess = [[sem(f"s_guess{s}{n}") for n in range(3)] for s in range(3)]
        s_started = sem("s_started")
        s_rank = sem("s_rank")
        s_below = sem("s_below")
        s_off = sem("s_off")
        s_thr = sem("s_thr")
        s_side = sem("s_side")
        s_dve_count = [sem(f"s_dve_count{n}") for n in range(3)]
        s_count = [[sem(f"s_count{s}{n}") for n in range(3)] for s in range(3)]
        s_bad = sem("s_bad")
        s_nbad = sem("s_nbad")
        s_redo = sem("s_redo")
        fast, general = Layer(sem, "fast"), Layer(sem, "general")

        STEP = (STEP_OUT, STEP_PROC, STEP_OUT)
        WIDTH = (N_IN, N_PROC, N_OUT)
        PAIRS = ((0, 1), (2, 3))
        NORM2 = ((0,), (1,), (2, 3))

        def on_dve(s, t):
            return s == 0 and t == 0

        def guess_at(s, n, t):
            j = s * TILES + t
            return guess[:, n, j:j + 1] if n < COUNTS[s] - 1 else ranked[:, j, 0:1]

        def count_there(eng, s, n, t):
            if on_dve(s, t):
                eng.wait_ge(s_dve_count[n], 1)
            else:
                eng.wait_ge(s_count[s][n], t + (s > 0))

        vr = par[:, C_PR:C_PR + 2 * STATE].rearrange("p (i n) -> p i n", i=2)
        pl = par[:, C_PL:C_PL + 2 * STATE].rearrange("p (i n) -> p i n", i=2)

        block = ctx.enter_context(nc.Block())

        @block.sync
        def _(sp):
            sp.dma_start(par[:, :], ssm).then_inc(s_par, 16)
            for c in range(2 * XG):
                sp.dma_start(xt[:, c, :, :], x_t[c]).then_inc(s_x[c], 16)
            sp.dma_start(ipt[:, :], ip_t).then_inc(s_ip, 16)
            sp.dma_start(piwt[:, :, :], piw_t).then_inc(s_piw, 16)
            sp.dma_start(pvs[:, :, :], pv).then_inc(s_pv, 16)
            sp.dma_start(oiwt[:, :], oiw_t).then_inc(s_oiw, 16)
            sp.dma_start(ops[:, :, :], op).then_inc(s_op, 16)

            def store(run):
                for tiles in ((0, 1), (2,), (3,)):
                    tokens = slice(tiles[0] * P, (tiles[-1] + 1) * P)
                    sp.wait_ge(run.result, tiles[-1] + 1)
                    sp.dma_start(out[:, tokens], o_sb[:, tokens]).then_inc(run.stored, 16)
                sp.wait_ge(run.stored, 48)

            store(fast)
            sp.wait_ge(s_redo, 1)
            with sp.If(sp.value_load(redo[0:1, 0:1]) != 0):
                store(general)

        @block.gpsimd
        def _(pool):
            G = nc.gpsimd
            G.memset(warm[:, :], 0.0).then_inc(s_warm, 1)
            G.memset(ident[:, :], 0.0).then_inc(s_zeroed, 1)
            G.memset(minus_half[:, :], -0.5).then_inc(s_const, 1)
            G.memset(tiny[:, :], TINY).then_inc(s_const, 1)
            G.memset(ones_col[:, :], 1.0).then_inc(s_const, 1)
            G.iota(iota[:, :], pattern=[[1, max(RANKS)]], base=0, channel_multiplier=0,
                   allow_small_or_imprecise_dtypes=True).then_inc(s_const, 1)
            pool.wait_ge(s_zeroed, 1)
            G.affine_select(out=ident[:, :], in_=ident[:, :], compare_op=ALU.not_equal, fill=1.0,
                            base=0, pattern=[[-1, P]], channel_multiplier=1).then_inc(s_const, 1)
            pool.wait_ge(s_const, 5)

            G.tensor_scalar(centre[:, :], ident[:, :], -1.0 / P, None, ALU.add).then_inc(s_const, 1)

            def norm1_std(n):
                rows = slice(2 * n, 2 * n + 2)
                pool.wait_ge(s_hsq, 2 * n + 2)
                G.tensor_scalar(var1[:, rows], hsq[:, rows], 1.0 / P, EPS, ALU.mult, ALU.add).then_inc(s_pool, 1)
                pool.wait_ge(s_pool, n + 1)
                G.tensor_tensor(rstd1[:, rows], var1[:, rows], minus_half[:, 0:2], ALU.pow).then_inc(s_std1, 1)

            pool.wait_ge(s_ig, 2)
            for i in range(2):
                G.tensor_tensor(yv[:, i, :], vr[:, i, :], ig[:, :], ALU.mult).then_inc(s_y, 1)
            G.tensor_tensor(a_diag[:, :], g_minus[:, :], ig[:, :], ALU.mult).then_inc(s_y, 1)
            pool.wait_ge(s_y, 3)
            G.tensor_tensor(decayed_y[:, :], a_diag[:, :], par[:, C_C:C_C + STATE], ALU.mult).then_inc(s_decayed_y, 1)
            for k in range(HALF):
                pool.wait_ge(s_state, k + 1)
                if k < HALF - 1:
                    G.tensor_tensor(decayed_x[:, :], a_diag[:, :], states[:, k, :], ALU.mult).then_inc(s_decayed_x, 1)
                if k:
                    pool.wait_ge(s_adjoint, k)
                    G.tensor_tensor(decayed_y[:, :], a_diag[:, :], adjoint[:, (k - 1) % 2, :],
                                    ALU.mult).then_inc(s_decayed_y, 1)
                G.tensor_tensor(cs[:, k, :], par[:, C_C:C_C + STATE], states[:, k, :], ALU.mult).then_inc(s_cs, 1)
                if k in NORM1_AT:
                    norm1_std(NORM1_AT.index(k))

            def norm2_std(tiles):
                rows = slice(tiles[0], tiles[-1] + 1)
                pool.wait_ge(s_var, tiles[-1] + 1)
                G.tensor_tensor(rstd[:, rows], vare[:, rows], minus_half[:, 0:len(tiles)],
                                ALU.pow).then_inc(s_rstd, len(tiles))

            def prepare(s, t):
                j = s * TILES + t
                width, density, aim = WIDTH[s], (0.3989 if s == 1 else DENSITY_OUT), (AIM_PROC if s == 1 else AIM_OUT)
                rate = STEP[s] / (2.0 * width * GAUSS_MEAN * width * density)
                mixed = any(on_dve(s, other) for other in PAIRS[t // 2])
                if on_dve(s, t):
                    tiles, factor, shift = slice(j, j + 1), 2 * rate, -2 * aim * rate
                elif mixed:
                    tiles, factor, shift = slice(j, j + 1), -rate, (width - 2 * aim) * rate
                else:
                    tiles, factor, shift = slice(j, j + 2), -rate, (width - 2 * aim) * rate
                G.tensor_scalar(slope[:, tiles], gsum[:, tiles], factor, 0.0, ALU.mult, ALU.add).then_inc(s_pool, 1)
                G.tensor_scalar(base[:, tiles], gsum[:, tiles], shift, 0.0, ALU.mult, ALU.add).then_inc(s_pool, 1)

            starts = [0]

            def first_guess(s, a_done, pair):
                for t in pair:
                    pool.wait_ge(a_done, t + 1)
                    if s != 1:
                        j = s * TILES + t
                        G.tensor_scalar(guess[:, 0, j:j + 1], gsum[:, j:j + 1], START_OUT[s // 2] / WIDTH[s], 0.0,
                                        ALU.mult, ALU.add).then_inc(s_guess[s][0], 1)
                    if on_dve(s, pair[0]) or t == pair[1]:
                        prepare(s, t if on_dve(s, pair[0]) else pair[0])
                    if on_dve(s, t):
                        norm2_std(NORM2[2])
                pool.wait_ge(s_pool, 4 + 2 * (2 * s + pair[0] // 2 + 1))

            def begin_at(s, n, tiles):
                rows = slice(s * TILES + tiles[0], s * TILES + tiles[-1] + 1)
                pool.wait_ge(s_guess[s][n], tiles[-1] + 1)
                G.tensor_tensor(start[:, n, rows], base[:, rows], guess[:, n, rows], ALU.add).then_inc(s_started, 1)
                starts[0] += 1

            def correct(s, n, pair):
                apart = on_dve(s, pair[0])
                if s == 1:
                    begin = base
                else:
                    begin = start[:, n, :]
                    if not apart:
                        begin_at(s, n, pair)
                for t in pair:
                    if apart:
                        begin_at(s, n, (t,))
                    if s != 1:
                        pool.wait_ge(s_started, starts[0])
                    j = s * TILES + t
                    count_there(pool, s, n, t)
                    G.tensor_scalar(guess_at(s, n + 1, t), counted[:, j, n:n + 1], slope[:, j:j + 1],
                                    begin[:, j:j + 1], ALU.mult, ALU.add).then_inc(s_guess[s][n + 1], 1)
                    if s == 1:
                        pool.wait_ge(s_guess[s][n + 1], 2 * t + 1)
                        G.tensor_scalar(guess_at(s, n + 1, t), guess_at(s, n + 1, t), TINY, None,
                                        ALU.max).then_inc(s_guess[s][n + 1], 1)

            def rank_of_kth(s, pair):
                k = K_PROC if s == 1 else K_OUT
                for t in pair:
                    count_there(pool, s, COUNTS[s] - 1, t)
                for t in pair:
                    j = s * TILES + t
                    if on_dve(s, t):
                        tiles, factor, shift = slice(j, j + 1), -1.0, float(k)
                    elif on_dve(s, pair[0]):
                        tiles, factor, shift = slice(j, j + 1), 0.5, k - WIDTH[s] / 2.0
                    elif t == pair[0]:
                        tiles, factor, shift = slice(j, j + 2), 0.5, k - WIDTH[s] / 2.0
                    else:
                        continue
                    last = G.tensor_scalar(rank[:, tiles], counted[:, tiles, COUNTS[s] - 1], factor, shift,
                                           ALU.mult, ALU.add)
                last.then_inc(s_rank, 1)

            first, second = PAIRS
            norm2_std(NORM2[0])
            norm2_std(NORM2[1])
            for pair in PAIRS:
                first_guess(0, s_g1, pair)
                for n in range(2):
                    correct(0, n, pair)
                rank_of_kth(0, pair)
            t = second[1]
            G.tensor_tensor(below[:, t, :], sign_out[:, t % 2, :], g1[:, t, :], ALU.mult).then_inc(s_below, 1)
            first_guess(1, fast.a_proc, first)
            correct(1, 0, first)
            rank_of_kth(1, first)
            first_guess(1, fast.a_proc, second)
            correct(1, 0, second)
            rank_of_kth(1, second)
            for pair in PAIRS:
                first_guess(2, fast.a_out, pair)
                for n in range(2):
                    correct(2, n, pair)
                rank_of_kth(2, pair)

        @block.scalar
        def _(act):
            A = nc.scalar
            act.dma_start(wt[:, :, :], w_t).then_inc(s_w, 16)
            act.wait_ge(s_par, 16)
            A.activation(el[:, :], par[:, C_L:C_L + STATE], ACT.Exp).then_inc(s_exp, 1)
            A.activation(dt[:, :], par[:, C_DT:C_DT + 1], ACT.Exp).then_inc(s_exp, 1)

            act.wait_ge(s_const, 6)
            A.activation(gelu_junk[:, :], tiny[:, :], ACT.Gelu).then_inc(s_gelu_table, 1)

            def diagonal(k, value):
                A.activation(tap_diag[:, k, :], ident[:, :], ACT.Copy, scale=value).then_inc(s_diag, 1)

            def tap(k):
                act.wait_ge(s_cs, k + 1)
                A.activation(csum[:, :], cs[:, k, :], ACT.Identity, accum_out=taps[:, k:k + 1]).then_inc(s_tap, 1)
                value = taps[:, k:k + 1]
                if k == 0:
                    act.wait_ge(s_tap, 1)
                    A.activation(tap0[:, :], taps[:, 0:1], ACT.Identity,
                                 bias=par[:, C_D:C_D + 1]).then_inc(s_tap, 1)
                    value = tap0[:, :]
                act.wait_ge(s_tap, k + 2)
                diagonal(k, value)

            def embedded(n):
                act.wait_ge(s_h, n + 1)
                A.activation(h_t[:, n * 2 * P:(n + 1) * 2 * P], ps_a[n][:, 0:2 * P], ACT.Identity,
                             bias=par[:, C_TB:C_TB + 1]).then_inc(s_ht, 1)

            def squares(n):
                act.wait_ge(s_htok, n + 1)
                for t in PAIRS[n]:
                    A.activation(norm_junk[:, t, :], ps_t[n][:, t % 2, :], ACT.Square,
                                 accum_out=hsq[:, t:t + 1]).then_inc(s_hsq, 1)

            def normed(n):
                act.wait_ge(s_std1, n + 1)
                for t in PAIRS[n]:
                    A.activation(xn[:, t, :], ps_t[n][:, t % 2, :], ACT.Copy,
                                 scale=rstd1[:, t:t + 1]).then_inc(s_xn, 1)

            def normed_t(n):
                act.wait_ge(s_xnp, n + 1)
                A.activation(xn_t[:, n * 2 * P:(n + 1) * 2 * P], ps_q[n][:, 0:2 * P], ACT.Copy).then_inc(s_xnt, 1)

            embedded(0)
            tap(0)
            squares(0)
            tap(1)
            normed(0)
            embedded(1)
            normed_t(0)
            squares(1)
            tap(2)
            normed(1)
            tap(3)
            normed_t(1)
            for k in range(4, HALF):
                tap(k)
            for k in range(HALF, DVE_DIAG):
                act.wait_ge(s_late_tap, k - HALF + 1)
                diagonal(k, taps[:, k:k + 1])
            act.wait_ge(s_ipc_z, 1)
            A.activation(ipc[:, :], ps_z[0][:, :], ACT.Copy).then_inc(s_ipc, 1)

            def count(s, n, t, src):
                j = s * TILES + t
                if s == 1 and n == 0:
                    at = tiny[:, 0:1]
                else:
                    act.wait_ge(s_guess[s][n], 2 * (t + 1) if s == 1 else t + 1)
                    at = guess_at(s, n, t)
                if n == 0 and t >= 2 and not on_dve(s, t - 2):
                    count_there(act, s, COUNTS[s] - 1, t - 2)
                elif n == 0 and t < 2 and s:
                    count_there(act, s - 1, COUNTS[s - 1] - 1, t + 2)
                    if s == 1:
                        act.wait_ge(s_below, 1)
                A.activation(sign_out[:, t % 2, 0:WIDTH[s]], src[:, t, :], ACT.Sign, scale=-1.0, bias=at,
                             accum_out=counted[:, j, n:n + 1]).then_inc(s_count[s][n], 1)

            def move_in(run, t):
                act.wait_ge(run.picked_in_t, t + 1)
                A.activation(rt[:, t % 2, :], ps_t[t % 2][:, :, :], ACT.Copy).then_inc(run.in_t, 1)

            def gelu_proc(run, t):
                act.wait_ge(run.z_proc, t + 1)
                j = TILES + t
                A.activation(g2[:, t, :], ps_q[t % 2][:, 0:N_PROC], ACT.Gelu,
                             accum_out=gsum[:, j:j + 1]).then_inc(run.a_proc, 1)

            def exp_proc(run, pair):
                act.wait_ge(run.top_proc, pair[1] + 1)
                rows = slice(pair[0], pair[1] + 1)
                A.mul(neg_max[:, rows], top8[:, rows, 0], -1.0).then_inc(run.neg_max, 1)
                act.wait_ge(run.neg_max, pair[0] // 2 + 1)
                for t in pair:
                    A.activation(e2[:, t, :], g2[:, t, :], ACT.Exp, bias=neg_max[:, t:t + 1]).then_inc(run.exp_proc, 1)

            def move_weights(run, t):
                act.wait_ge(run.weights_t, t + 1)
                A.activation(rt[:, t % 2, 0:N_PROC], ps_t[t % 2][:, 0:2, :], ACT.Copy).then_inc(run.w_t, 1)

            def move_agg(run, t):
                act.wait_ge(run.agg, t + 1)
                A.activation(agg_t[:, t, :], ps_q[t % 2][0:D_PV, 0:P], ACT.Copy).then_inc(run.agg_sb, 1)

            def gelu_out(run, t):
                act.wait_ge(run.z_out, t + 1)
                act.wait_ge(run.inv_sum, t + 1)
                j = 2 * TILES + t
                A.activation(g3[:, t, :], ps_z[t % 2][:, :], ACT.Gelu, scale=inv_sum[:, t:t + 1],
                             accum_out=gsum[:, j:j + 1]).then_inc(run.a_out, 1)

            def move_out(run, t):
                act.wait_ge(run.picked_out_t, t + 1)
                A.activation(rt3[:, :, t * P:(t + 1) * P], ps_t[t % 2][:, :, :], ACT.Copy).then_inc(run.out_t, 1)

            def gelu_in(t):
                act.wait_ge(s_z1, t + 1)
                act.wait_ge(s_rstd, t + 1)
                A.activation(g1[:, t, :], ps_z[t % 2][:, :], ACT.Gelu, scale=rstd[:, t:t + 1],
                             accum_out=gsum[:, t:t + 1]).then_inc(s_g1, 1)

            gelu_in(0)
            gelu_in(1)
            act.wait_ge(s_g1, 2)
            count(0, 0, 1, g1)
            gelu_in(2)
            count(0, 1, 1, g1)
            gelu_in(3)
            count(0, 2, 1, g1)
            act.wait_ge(s_g1, TILES)
            for n in range(3):
                for t in PAIRS[1]:
                    count(0, n, t, g1)
            count_there(act, 0, 2, TILES - 1)
            A.activation(off_junk[:, :], sign_out[:, 1, :], ACT.Square, accum_out=off_guess[:, :]).then_inc(s_off, 1)

            first, second = PAIRS

            def counts(s, n, pair, src, src_ready):
                for t in pair:
                    if n == 0:
                        act.wait_ge(src_ready, t + 1)
                    count(s, n, t, src)

            def aggregate(run, pair):
                for t in pair:
                    move_weights(run, t)
                for t in pair:
                    move_agg(run, t)
                for t in pair:
                    gelu_out(run, t)

            for t in first:
                move_in(fast, t)
            def side(t):
                act.wait_ge(s_thr, t + 1)
                A.activation(side2[:, t, :], g2[:, t, :], ACT.Sign, scale=-1.0, bias=thr[:, TILES + t:TILES + t + 1],
                             accum_out=sides2[:, t:t + 1]).then_inc(s_side, 1)

            for t in first:
                gelu_proc(fast, t)
            counts(1, 0, first, g2, fast.a_proc)
            for t in second:
                move_in(fast, t)
            counts(1, 1, first, g2, fast.a_proc)
            for t in second:
                gelu_proc(fast, t)
            counts(1, 0, second, g2, fast.a_proc)
            for t in first:
                side(t)
            for pair in PAIRS:
                exp_proc(fast, pair)
            act.wait_ge(s_gelu_table, 1)
            A.activation(gelu_junk[:, :], tiny[:, :], ACT.Gelu).then_inc(s_gelu_table, 1)
            for t in first:
                move_weights(fast, t)
            counts(1, 1, second, g2, fast.a_proc)
            for t in first:
                move_agg(fast, t)
            gelu_out(fast, first[0])
            for t in second:
                side(t)
            gelu_out(fast, first[1])
            for n in range(2):
                counts(2, n, first, g3, fast.a_out)
            for t in second:
                move_weights(fast, t)
            count(2, 2, first[0], g3)
            for t in second:
                move_agg(fast, t)
            count(2, 2, first[1], g3)
            for t in second:
                gelu_out(fast, t)
            counts(2, 0, second, g3, fast.a_out)
            counts(2, 1, second, g3, fast.a_out)
            for t in first:
                move_out(fast, t)
            counts(2, 2, second, g3, fast.a_out)
            for t in second:
                move_out(fast, t)

            act.wait_ge(s_redo, 1)
            with act.If(act.value_load(redo[0:1, 0:1]) != 0):
                for pair in PAIRS:
                    for t in pair:
                        move_in(general, t)
                    for t in pair:
                        gelu_proc(general, t)
                for pair in PAIRS:
                    exp_proc(general, pair)
                for pair in PAIRS:
                    aggregate(general, pair)
                for t in range(TILES):
                    move_out(general, t)

        @block.vector
        def _(dve):
            V = nc.vector
            steps = [0]

            def step(ins):
                ins.then_inc(s_dve, 1)
                steps[0] += 1
                return steps[0]

            def after_step(n):
                dve.wait_ge(s_dve, n)

            def dot(out_, u, v, j):
                return V.scalar_tensor_tensor(out=junk[:, j, :], in0=u, scalar=1.0, in1=v, op0=ALU.mult,
                                              op1=ALU.mult, accum_out=out_)

            dve.wait_ge(s_par, 16)
            dve.wait_ge(s_exp, 2)
            n = step(V.tensor_scalar(hdt[:, :], dt[:, :], 0.5, None, ALU.mult))
            after_step(n)
            n = step(V.tensor_scalar(g[:, :], el[:, :], hdt[:, 0:1], None, ALU.mult))
            after_step(n)
            n = step(V.tensor_scalar(g_plus[:, :], g[:, :], 1.0, None, ALU.add))
            V.tensor_scalar(g_minus[:, :], g[:, :], -1.0, 1.0, ALU.mult, ALU.add).then_inc(s_ig, 1)
            after_step(n)
            V.reciprocal(ig[:, :], g_plus[:, :]).then_inc(s_ig, 1)
            dve.wait_ge(s_ig, 2)
            for i in range(2):
                n = step(V.scalar_tensor_tensor(out=xu[:, i, :], in0=pl[:, i, :], scalar=hdt[:, 0:1], in1=ig[:, :],
                                                op0=ALU.mult, op1=ALU.mult))
            m = step(V.scalar_tensor_tensor(out=bi[:, :], in0=par[:, C_B:C_B + STATE], scalar=dt[:, 0:1],
                                            in1=ig[:, :], op0=ALU.mult, op1=ALU.mult))
            after_step(n)
            for i in range(2):
                for j in range(2):
                    n = step(dot(vx[:, 2 * i + j:2 * i + j + 1], vr[:, i, :], xu[:, j, :], 2 * i + j))
            after_step(m)
            for i in range(2):
                m = step(dot(bdot[:, i:i + 1], vr[:, i, :], bi[:, :], 4 + i))
            after_step(n)
            n = step(V.tensor_scalar(one_minus[:, :], vx[:, :], -1.0, 1.0, ALU.mult, ALU.add))
            step(V.tensor_tensor(det[:, 0:1], vx[:, 1:2], vx[:, 2:3], ALU.mult))
            after_step(n + 1)
            n = step(V.scalar_tensor_tensor(out=det[:, 1:2], in0=one_minus[:, 0:1], scalar=one_minus[:, 3:4],
                                            in1=det[:, 0:1], op0=ALU.mult, op1=ALU.subtract))
            step(V.tensor_scalar(half_bdot[:, :], bdot[:, :], 0.5, None, ALU.mult))
            after_step(n)
            n = step(V.reciprocal(det[:, 2:3], det[:, 1:2]))
            after_step(n)
            step(V.tensor_scalar(own[:, :], one_minus[:, :], det[:, 2:3], 2.0, ALU.mult, ALU.mult))
            n = step(V.tensor_scalar(other[:, :], vx[:, :], det[:, 2:3], 2.0, ALU.mult, ALU.mult))
            after_step(n)
            step(V.tensor_scalar(xs[:, 0, :], xu[:, 0, :], own[:, 3:4], None, ALU.mult))
            n = step(V.tensor_scalar(xs[:, 1, :], xu[:, 1, :], own[:, 0:1], None, ALU.mult))
            after_step(n - 1)
            step(V.scalar_tensor_tensor(out=xf[:, 0, :], in0=xu[:, 1, :], scalar=other[:, 2:3], in1=xs[:, 0, :],
                                        op0=ALU.mult, op1=ALU.add))
            after_step(n)
            n = step(V.scalar_tensor_tensor(out=xf[:, 1, :], in0=xu[:, 0, :], scalar=other[:, 1:2], in1=xs[:, 1, :],
                                            op0=ALU.mult, op1=ALU.add))
            after_step(n - 1)
            n = step(V.scalar_tensor_tensor(out=half_x[:, :], in0=xf[:, 0, :], scalar=half_bdot[:, 0:1],
                                            in1=bi[:, :], op0=ALU.mult, op1=ALU.add))
            def dots(out_, m, v, j):
                for i in range(2):
                    n = step(dot(out_[:, i:i + 1], m[:, i, :], v, j + i))
                return n

            after_step(n - 1)
            done_y = dots(udot, xf, par[:, C_C:C_C + STATE], 2)
            after_step(n)
            V.scalar_tensor_tensor(out=states[:, 0, :], in0=xf[:, 1, :], scalar=half_bdot[:, 1:2],
                                   in1=half_x[:, :], op0=ALU.mult, op1=ALU.add).then_inc(s_state, 1)
            dve.wait_ge(s_y, 3)
            for k in range(HALF):
                more_x = k < HALF - 1
                if more_x:
                    dve.wait_ge(s_state, k + 1)
                    done_x = dots(wdot, yv, states[:, k, :], 6)
                if k:
                    dve.wait_ge(s_adjoint, k)
                    done_y = dots(udot, xf, adjoint[:, (k - 1) % 2, :], 2)
                if more_x:
                    after_step(done_x)
                    dve.wait_ge(s_decayed_x, k + 1)
                    half_x_at = step(V.scalar_tensor_tensor(out=half_x[:, :], in0=xf[:, 0, :], scalar=wdot[:, 0:1],
                                                            in1=decayed_x[:, :], op0=ALU.mult, op1=ALU.add))
                after_step(done_y)
                dve.wait_ge(s_decayed_y, k + 1)
                half_y_at = step(V.scalar_tensor_tensor(out=half_y[:, :], in0=yv[:, 0, :], scalar=udot[:, 0:1],
                                                        in1=decayed_y[:, :], op0=ALU.mult, op1=ALU.add))
                if more_x:
                    after_step(half_x_at)
                    V.scalar_tensor_tensor(out=states[:, k + 1, :], in0=xf[:, 1, :], scalar=wdot[:, 1:2],
                                           in1=half_x[:, :], op0=ALU.mult, op1=ALU.add).then_inc(s_state, 1)
                after_step(half_y_at)
                V.scalar_tensor_tensor(out=adjoint[:, k % 2, :], in0=yv[:, 1, :], scalar=udot[:, 1:2],
                                       in1=half_y[:, :], op0=ALU.mult, op1=ALU.add).then_inc(s_adjoint, 1)
            dve.wait_ge(s_adjoint, HALF)
            for k in range(HALF, TAPS):
                dot(taps[:, k:k + 1], adjoint[:, (HALF - 1) % 2, :], states[:, k - HALF, :],
                    k - HALF).then_inc(s_late_tap, 1)
            dve.wait_ge(s_const, 6)
            for k in range(DVE_DIAG, TAPS):
                dve.wait_ge(s_late_tap, k - HALF + 1)
                V.tensor_scalar(tap_diag[:, k, :], ident[:, :], taps[:, k:k + 1], None,
                                ALU.mult).then_inc(s_late_diag, 1)
            dve.wait_ge(s_conv, 1)
            for tiles in NORM2:
                tokens = slice(tiles[0] * P, (tiles[-1] + 1) * P)
                V.tensor_tensor(h2_t[:, tokens], ps_c[:, tokens], h_t[:, tokens], ALU.add).then_inc(s_h2, len(tiles))
            for tiles in NORM2:
                dve.wait_ge(s_h2tok, tiles[-1] + 1)
                for t in tiles:
                    m = step(V.bn_stats(out=stats[:, t, :], in_=ps_norm2[t][:, 0:P]))
                for t in tiles:
                    after_step(m - (tiles[-1] - t))
                    k = step(V.bn_aggr(out=mv[:, t, :], in_=stats[:, t, :]))
                after_step(k)
                rows = slice(tiles[0], tiles[-1] + 1)
                V.tensor_scalar(vare[:, rows], mv[:, rows, 1], EPS, None, ALU.add).then_inc(s_var, len(tiles))

            def count_above(s, n, t, src):
                j = s * TILES + t
                dve.wait_ge(s_guess[s][n], t + 1)
                V.tensor_scalar(above_out[:, :], src[:, t, :], guess_at(s, n, t), None, ALU.is_gt, ALU.add,
                                accum_out=counted[:, j, n:n + 1]).then_inc(s_dve_count[n], 1)

            def candidates(s, pair, src, parts):
                width = WIDTH[s]
                size = width // parts
                done = {}
                cand = cands[s]
                for t in pair:
                    if s == 0 and t == TILES - 1:
                        dve.wait_ge(s_below, 1)
                        done[t] = 0
                    else:
                        dve.wait_ge(s_guess[s][COUNTS[s] - 1], 2 * (t + 1) if s == 1 else t + 1)
                        done[t] = step(V.scalar_tensor_tensor(out=below[:, t, 0:width], in0=src[:, t, :],
                                                              scalar=guess_at(s, COUNTS[s] - 1, t), in1=src[:, t, :],
                                                              op0=ALU.is_le, op1=ALU.mult))
                for t in pair:
                    if done[t]:
                        after_step(done[t])
                    for q in range(parts):
                        done[t] = step(V.max(out=cand[:, t, 8 * q:8 * q + 8],
                                             in_=below[:, t, q * size:(q + 1) * size]))
                held = {t: cand for t in pair}
                for r in range(RANKS[s] // 8):
                    for t in pair:
                        j = s * TILES + t
                        after_step(done[t])
                        done[t] = step(V.max(out=ranked[:, j, 1 + 8 * r:9 + 8 * r], in_=held[t][:, t, 0:8 * parts]))
                    if r < RANKS[s] // 8 - 1:
                        for t in pair:
                            j = s * TILES + t
                            after_step(done[t])
                            source, held[t] = held[t], cand_left[r]
                            done[t] = step(V.match_replace(out=held[t][:, t, 0:8 * parts],
                                                           in_to_replace=ranked[:, j, 1 + 8 * r:9 + 8 * r],
                                                           in_values=source[:, t, 0:8 * parts], imm_value=LOW))

            def threshold(s, pair):
                dve.wait_ge(s_rank, 2 * s + pair[0] // 2 + 1)
                after_step(steps[0])
                for t in pair:
                    j = s * TILES + t
                    pick = V.scalar_tensor_tensor(out=pick_a[:, t, 0:RANKS[s]], in0=iota[:, 0:RANKS[s]],
                                                  scalar=rank[:, j:j + 1], in1=ranked[:, j, 0:RANKS[s]],
                                                  op0=ALU.is_equal, op1=ALU.mult, accum_out=thr[:, j:j + 1])
                    if s == 1:
                        pick.then_inc(s_thr, 1)
                    else:
                        m = step(pick)
                if s != 1:
                    for t in pair:
                        j = s * TILES + t
                        step(V.scalar_tensor_tensor(out=pick_b[:, t, 0:RANKS[s]], in0=iota[:, 0:RANKS[s]],
                                                    scalar=rank[:, j:j + 1], in1=ranked[:, j, 1:RANKS[s] + 1],
                                                    op0=ALU.is_equal, op1=ALU.mult, accum_out=after[:, j:j + 1]))
                    after_step(m)

            def prove_patterns(s):
                rows = slice(s * TILES, (s + 1) * TILES)
                at = 3 * (s // 2)
                after_step(steps[0])
                n = step(V.tensor_reduce(out=last8[:, rows], in_=cands[s][:, :, 7:8 * PARTS:8],
                                         axis=AX.X, op=ALU.max))
                step(V.tensor_tensor(proofs[:, at, :], ranked[:, rows, 1], ranked[:, rows, 0], ALU.is_lt))
                step(V.tensor_tensor(proofs[:, at + 1, :], after[:, rows], thr[:, rows], ALU.is_lt))
                after_step(n)
                if s == 0:
                    dve.wait_ge(s_off, 1)
                    after_step(n + 1)
                    step(V.scalar_tensor_tensor(out=proofs[:, 0, TILES - 1:], in0=off_guess[:, :], scalar=float(N_IN),
                                                in1=proofs[:, 0, TILES - 1:], op0=ALU.is_ge, op1=ALU.mult))
                step(V.tensor_tensor(proofs[:, at + 2, :], last8[:, rows], thr[:, rows], ALU.is_lt))

            def prove_process():
                step(V.tensor_scalar(proofs[:, 6, :], n_tied2[:, :], 0.0, None, ALU.is_ge))
                step(V.tensor_tensor(proofs[:, 7, :], order2[:, :, N_PROC - 1], n_tied2[:, :], ALU.is_ge))

            def keep_largest(s, pair, src, done):
                candidates(s, pair, src, PARTS)
                threshold(s, pair)
                for t in pair:
                    j = s * TILES + t
                    V.scalar_tensor_tensor(out=r1[:, t, :], in0=src[:, t, :], scalar=thr[:, j:j + 1],
                                           in1=src[:, t, :], op0=ALU.is_ge, op1=ALU.mult).then_inc(done, 1)

            def finish_weights(run, tiles, mask, scalar, op0):
                for t in tiles:
                    dve.wait_ge(run.exp_proc, t + 1)
                    V.scalar_tensor_tensor(out=p2[:, t, :], in0=mask(t), scalar=scalar, in1=e2[:, t, :],
                                           op0=op0, op1=ALU.mult, accum_out=sum_p[:, t:t + 1]).then_inc(run.weights, 1)
                dve.wait_ge(run.weights, t + 1)
                rows = slice(tiles[0], t + 1)
                V.reciprocal(inv_sum[:, rows], sum_p[:, rows]).then_inc(run.inv_sum, len(tiles))

            for n in range(3):
                count_above(0, n, 0, g1)
            for pair in PAIRS:
                keep_largest(0, pair, g1, fast.picked_in)

            def row_maxima(pair):
                for t in pair:
                    dve.wait_ge(fast.a_proc, t + 1)
                    V.max(out=top8[:, t, :], in_=g2[:, t, :]).then_inc(fast.top_proc, 1)

            row_maxima(PAIRS[0])
            for pair in PAIRS:
                candidates(1, pair, g2, PARTS)
                threshold(1, pair)
                if pair == PAIRS[0]:
                    row_maxima(PAIRS[1])
                else:
                    prove_patterns(0)
                for t in pair:
                    dve.wait_ge(s_side, t + 1)
                    n = step(V.tensor_scalar(equal2[:, t, :], side2[:, t, :], 0.0, None, ALU.is_equal))
                rows = slice(pair[0], pair[1] + 1)
                step(V.tensor_scalar(half_sides2[:, rows], sides2[:, rows], 0.5, K_PROC - N_PROC / 2.0,
                                     ALU.mult, ALU.add))
                for t in pair:
                    after_step(n - (pair[1] - t))
                    m = step(V.tensor_tensor_scan(order2[:, t, :], equal2[:, t, :], equal2[:, t, :],
                                                  0.0, ALU.add, ALU.max))
                after_step(m)
                n = step(V.scalar_tensor_tensor(out=n_tied2[:, rows], in0=order2[:, rows, N_PROC - 1], scalar=0.5,
                                                in1=half_sides2[:, rows], op0=ALU.mult, op1=ALU.add))
                after_step(n)
                for t in pair:
                    n = step(V.scalar_tensor_tensor(out=mask2[:, t, :], in0=order2[:, t, :],
                                                    scalar=n_tied2[:, t:t + 1], in1=side2[:, t, :],
                                                    op0=ALU.is_le, op1=ALU.subtract))
                after_step(n)
                finish_weights(fast, pair, lambda t: mask2[:, t, :], 0.0, ALU.is_gt)
            prove_process()
            for pair in PAIRS:
                keep_largest(2, pair, g3, fast.picked_out)

            def results(run, pair):
                for t in pair:
                    tokens = slice(t * P, (t + 1) * P)
                    dve.wait_ge(run.y, t + 1)
                    V.tensor_tensor(o_sb[:, tokens], ps_y[t % 2][:, 0:P], h2_t[:, tokens],
                                    ALU.add).then_inc(run.result, 1)

            results(fast, PAIRS[0])
            prove_patterns(2)
            after_step(steps[0])
            n = step(V.tensor_reduce(out=good[:, :], in_=proofs[:, :, :], axis=AX.XY, op=ALU.min))
            after_step(n)
            V.tensor_scalar(bad[:, :], good[:, :], -1.0, 1.0, ALU.mult, ALU.add).then_inc(s_bad, 1)
            results(fast, PAIRS[1])
            dve.wait_ge(s_nbad, 1)
            V.tensor_copy(redo[:, :], ps_q[1][0:1, 0:1]).then_inc(s_redo, 1)

            dve.wait_ge(s_redo, 1)
            with dve.If(dve.value_load(redo[0:1, 0:1]) != 0):
                def mark_largest(src, width, k):
                    for r in range(k // 8):
                        now = src if r == 0 else left[:, 0:width]
                        n = step(V.max(out=v8[:, :], in_=now))
                        after_step(n)
                        n = step(V.match_replace(out=left[:, 0:width], in_to_replace=v8[:, :], in_values=now,
                                                 imm_value=LOW))
                        after_step(n)

                def keep_marked(src, t, done):
                    V.scalar_tensor_tensor(out=r1[:, t, :], in0=left[:, :], scalar=PICKED, in1=src[:, t, :],
                                           op0=ALU.is_le, op1=ALU.mult).then_inc(done, 1)
                    dve.wait_ge(done, t + 1)

                for t in range(TILES):
                    mark_largest(g1[:, t, :], N_IN, K_IN)
                    keep_marked(g1, t, general.picked_in)
                for t in range(TILES):
                    dve.wait_ge(general.a_proc, t + 1)
                    V.max(out=top8[:, t, :], in_=g2[:, t, :]).then_inc(general.top_proc, 1)
                for t in range(TILES):
                    mark_largest(g2[:, t, :], N_PROC, K_PROC)
                    finish_weights(general, (t,), lambda t: left[:, 0:N_PROC], PICKED, ALU.is_le)
                for t in range(TILES):
                    dve.wait_ge(general.a_out, t + 1)
                    mark_largest(g3[:, t, :], N_OUT, K_OUT)
                    keep_marked(g3, t, general.picked_out)
                dve.wait_ge(fast.stored, 48)
                results(general, range(TILES))

        @block.tensor
        def _(pe):
            T = nc.tensor
            def keep_warm(products):
                for _ in range(products):
                    last = T.matmul(ps_h[:, 0:P], warm[:, 0:P], warm[:, 0:P], start=True, stop=True)
                last.then_inc(s_warmed, 1)

            pe.wait_ge(s_warm, 1)
            keep_warm(WARM)
            pe.wait_ge(s_warmed, 1)
            pe.wait_ge(s_w, 16)

            def embed(n, groups):
                for c in groups:
                    pe.wait_ge(s_x[n * XG + c], 16)
                    for i in range(KC // XG):
                        k = c * (KC // XG) + i
                        last = T.matmul(ps_a[n][:, 0:2 * P], wt[:, k, :], xt[:, n * XG + c, i, :],
                                        start=(k == 0), stop=(k == KC - 1))
                if k == KC - 1:
                    last.then_inc(s_h, 1)

            def tokens_in_front(n):
                pe.wait_ge(s_ht, n + 1)
                for t in PAIRS[n]:
                    last = T.matmul(ps_t[n][:, t % 2, :], h_t[:, t * P:(t + 1) * P], centre[:, :], start=True,
                                    stop=True)
                last.then_inc(s_htok, 1)

            embed(0, range(XG))
            embed(1, range(1))
            pe.wait_ge(s_const, 6)
            tokens_in_front(0)
            embed(1, range(1, XG))
            T.matmul(ps_c[:, :], warm[:, 0:P], warm[:, :], start=True, stop=False).then_inc(s_opened, 1)

            def channels_in_front(n):
                pe.wait_ge(s_xn, 2 * n + 2)
                for t in PAIRS[n]:
                    last = T.transpose(ps_q[n][:, (t % 2) * P:(t % 2 + 1) * P], xn[:, t, :], ident[:, :])
                last.then_inc(s_xnp, 1)

            def convolve(first, images, taps_now):
                tokens = slice(first * PATCHES, (first + images) * PATCHES)
                src = xn_t[:, tokens].rearrange("p (b n) -> p b n", b=images)
                dst = ps_c[:, tokens].rearrange("p (b n) -> p b n", b=images)
                for k in taps_now:
                    if k < DVE_DIAG:
                        pe.wait_ge(s_diag, k + 1)
                    else:
                        pe.wait_ge(s_late_diag, k - DVE_DIAG + 1)
                    last = T.matmul(dst[:, :, k:], tap_diag[:, k, :], src[:, :, 0:PATCHES - k],
                                    start=False, stop=(k == TAPS - 1))
                return last

            channels_in_front(0)
            tokens_in_front(1)
            pe.wait_ge(s_xnt, 1)
            pe.wait_ge(s_opened, 1)
            convolve(0, BATCH // 2, range(2))
            pe.wait_ge(s_ip, 16)
            T.matmul(ps_z[0][:, :], centre[:, :], ipt[:, :], start=True, stop=True).then_inc(s_ipc_z, 1)
            channels_in_front(1)
            convolve(0, BATCH // 2, range(2, FIRST_TAPS))
            pe.wait_ge(s_xnt, 2)
            convolve(BATCH // 2, BATCH // 2, range(FIRST_TAPS))
            convolve(0, BATCH, range(FIRST_TAPS, TAPS)).then_inc(s_conv, 1)
            def norm2_tokens(tiles):
                for t in tiles:
                    pe.wait_ge(s_h2, t + 1)
                    T.transpose(ps_norm2[t][:, 0:P], h2_t[:, t * P:(t + 1) * P], ident[:, :]).then_inc(s_h2tok, 1)

            def match_input(t):
                if t >= 2:
                    pe.wait_ge(s_g1, t - 1)
                T.matmul(ps_z[t % 2][:, :], h2_t[:, t * P:(t + 1) * P], ipc[:, :], start=True,
                         stop=True).then_inc(s_z1, 1)

            norm2_tokens((0, 1))
            pe.wait_ge(s_ipc, 1)
            match_input(0)
            norm2_tokens((2, 3))
            for t in range(1, TILES):
                match_input(t)

            def transposes(src, t, chunks, done):
                for c in range(chunks):
                    last = T.transpose(ps_t[t % 2][:, c, :], src[:, t, c * P:(c + 1) * P], ident[:, :])
                last.then_inc(done, 1)

            def layer(run):
                pe.wait_ge(s_piw, 16)
                warmed = run is fast
                if warmed:
                    keep_warm(WARM_LAYER[0])
                    for n in (1, 2):
                        count_there(pe, 0, n, 1)
                        keep_warm(WARM_LAYER[0])
                    for n in range(COUNTS[0]):
                        count_there(pe, 0, n, 2)
                        keep_warm(WARM_LAYER[0])
                for n, pair in enumerate(PAIRS):
                    if warmed and n:
                        keep_warm(WARM_LAYER[1])
                    for t in pair:
                        pe.wait_ge(run.picked_in, t + 1)
                        if t >= 2:
                            pe.wait_ge(run.in_t, t - 1)
                        transposes(r1, t, N_IN // P, run.picked_in_t)
                    for t in pair:
                        pe.wait_ge(run.in_t, t + 1)
                        if t >= 2:
                            pe.wait_ge(run.a_proc, t - 1)
                        for c in range(N_IN // P):
                            last = T.matmul(ps_q[t % 2][:, 0:N_PROC], rt[:, t % 2, c * P:(c + 1) * P],
                                            piwt[:, c, :], start=(c == 0), stop=(c == N_IN // P - 1))
                        last.then_inc(run.z_proc, 1)
                pe.wait_ge(s_pv, 16)
                pe.wait_ge(s_oiw, 16)
                if warmed:
                    keep_warm(WARM_LAYER[2])
                    pe.wait_ge(fast.top_proc, TILES)
                for n, pair in enumerate(PAIRS):
                    if warmed:
                        keep_warm(WARM_LAYER[3 + n])
                    for t in pair:
                        pe.wait_ge(run.weights, t + 1)
                        if t >= 2:
                            pe.wait_ge(run.w_t, t - 1)
                        transposes(p2, t, N_PROC // P, run.weights_t)
                    if warmed:
                        keep_warm(5)
                    pe.wait_ge(run.a_proc, TILES)
                    for t in pair:
                        pe.wait_ge(run.w_t, t + 1)
                        if t >= 2:
                            pe.wait_ge(run.agg_sb, t - 1)
                        for c in range(N_PROC // P):
                            last = T.matmul(ps_q[t % 2][0:D_PV, 0:P], pvs[:, c, :],
                                            rt[:, t % 2, c * P:(c + 1) * P],
                                            start=(c == 0), stop=(c == N_PROC // P - 1))
                        last.then_inc(run.agg, 1)
                    if warmed:
                        keep_warm(1)
                    for t in pair:
                        pe.wait_ge(run.agg_sb, t + 1)
                        if t >= 2:
                            pe.wait_ge(run.a_out, t - 1)
                        T.matmul(ps_z[t % 2][:, :], agg_t[:, t, :], oiwt[:, :], start=True,
                                 stop=True).then_inc(run.z_out, 1)
                pe.wait_ge(s_op, 16)
                for n, pair in enumerate(PAIRS):
                    if warmed:
                        keep_warm(WARM_LAYER[5 + n])
                    for t in pair:
                        pe.wait_ge(run.picked_out, t + 1)
                        if t >= 2:
                            pe.wait_ge(run.out_t, t - 1)
                        transposes(r1, t, N_OUT // P, run.picked_out_t)
                    for t in pair:
                        pe.wait_ge(run.out_t, t + 1)
                        if t >= 2:
                            pe.wait_ge(run.result, t - 1)
                        for c in range(N_OUT // P):
                            last = T.matmul(ps_y[t % 2][:, 0:P], ops[:, c, :], rt3[:, c, t * P:(t + 1) * P],
                                            start=(c == 0), stop=(c == N_OUT // P - 1))
                        last.then_inc(run.y, 1)

            layer(fast)
            pe.wait_ge(s_bad, 1)
            T.matmul(ps_q[1][0:1, 0:1], bad[:, :], ones_col[:, :], start=True, stop=True).then_inc(s_nbad, 1)
            pe.wait_ge(s_redo, 1)
            with pe.If(pe.value_load(redo[0:1, 0:1]) != 0):
                layer(general)


def kernel(**inputs):
    import numpy as np
    import concourse.bacc as bacc
    from concourse.bass_utils import run_bass_kernel_spmd

    a = {k: np.asarray(v) for k, v in inputs.items()}
    xp = a["x"].reshape(BATCH, 3, 4, 16, 4, 16).transpose(1, 3, 5, 0, 2, 4).reshape(KC, P, TILES, P)
    arrays = {
        "x_t": xp.reshape(XG, KC // XG, P, 2, 2 * P).transpose(3, 0, 2, 1, 4).reshape(2 * XG, P, KC // XG, 2 * P),
        "w_t": a["L0_tok_W"].T.reshape(KC, P, P).transpose(1, 0, 2),
        "ssm": np.concatenate([a["L0_attn_L_param"], a["L0_attn_P_left"].transpose(0, 2, 1).reshape(P, -1),
                               a["L0_attn_P_right"].reshape(P, -1), a["L0_attn_B"], a["L0_attn_C"],
                               a["L0_attn_D"].reshape(P, 1), a["L0_attn_log_dt"], a["L0_tok_b"].reshape(P, 1)], axis=1),
        "ip_t": a["L0_ffn_input_patterns"].T,
        "piw_t": a["L0_ffn_process_input_weights"].T.reshape(N_IN // P, P, N_PROC).transpose(1, 0, 2),
        "pv": a["L0_ffn_process_values"].reshape(N_PROC // P, P, D_PV).transpose(1, 0, 2),
        "oiw_t": a["L0_ffn_output_input_weights"].T,
        "op": a["L0_ffn_output_patterns"].reshape(N_OUT // P, P, P).transpose(1, 0, 2),
    }
    arrays = {k: np.ascontiguousarray(v) for k, v in arrays.items()}
    nc = bacc.Bacc("TRN2", target_bir_lowering=False, num_devices=1)
    aps = [nc.dram_tensor(k, v.shape, mybir.dt.from_np(v.dtype), kind="ExternalInput").ap()
           for k, v in arrays.items()]
    out = nc.dram_tensor("out", (P, TOK), FP32, kind="ExternalOutput").ap()
    build(nc, *aps, out)
    r = run_bass_kernel_spmd(nc, [arrays], core_ids=[0])
    return r.results[0]["out"].T.reshape(BATCH, PATCHES, P)
```
